# Optimizing a Trainium2 kernel written in Bass

```python
import numpy as np
import jax
import jax.numpy as jnp

def _softmax(x, axis=-1):
    return jax.nn.softmax(x, axis=axis)

def _gelu(x):
    return jax.nn.gelu(x, approximate=True)

def _silu(x):
    return jax.nn.silu(x)

def _sigmoid(x):
    return jax.nn.sigmoid(x)

def _layernorm(x, axis=-1, eps=1e-05):
    m = jnp.mean(x, axis=axis, keepdims=True)
    v = jnp.var(x, axis=axis, keepdims=True)
    return (x - m) / jnp.sqrt(v + eps)

def _scatter_add(tgt, idx, src, axis=0):
    return tgt.at[idx].add(src)

def _segment_sum(src, seg, n):
    return jax.ops.segment_sum(src, seg, n)
kernel_name = 'mk_decoder_preln_d1_seqx_r4_61b5e3'

def setup_inputs(seed: int=0):
    np.random.seed(seed)
    _w = jnp.asarray

    def _rec_inputs():
        import jax
        import jax.numpy as jnp
        _rk = jax.random.key(seed)
        x = 7.22e-05 + 1 * jax.random.normal(jax.random.fold_in(_rk, 1), (16, 256, 256), jnp.float32)
        _lenS = 256 - jax.random.randint(jax.random.fold_in(_rk, 7), (16,), 0, max(1, 256 // 4) + 1, jnp.int32)
        _lenS2 = 256 - jax.random.randint(jax.random.fold_in(_rk, 8), (16,), 0, max(1, 256 // 4) + 1, jnp.int32)
        _ctx_1024P = jax.random.normal(jax.random.fold_in(_rk, 11), (16, 16, 256), jnp.float32)
        _ctx_1024c = jax.random.dirichlet(jax.random.fold_in(_rk, 511), 0.3 * jnp.ones((16,), jnp.float32), (16, 256))
        _ctx_1024t = jnp.einsum('bsk,bkd->bsd', _ctx_1024c, _ctx_1024P)
        _ctx_1024t = _ctx_1024t * jax.lax.rsqrt(jnp.mean(jnp.square(_ctx_1024t)) + 1e-12) * 0.953939
        ctx_1024 = 4.13588e-05 + 0.999923 * (_ctx_1024t + 0.3 * jax.random.normal(jax.random.fold_in(_rk, 611), (16, 256, 256), jnp.float32))
        return (x, ctx_1024)
    x, ctx_1024 = _rec_inputs()

    def _L0_attn_setup():
        import jax, jax.numpy as jnp
        import numpy as np
        B, S, D = (4, 1024, 256)
        key = jax.random.key(seed)
        ks = jax.random.split(key, 7)
        scale = 1.0 / np.sqrt(D)
        return {'x': jax.random.normal(ks[0], (B, S, D), dtype=jnp.float32), 'Wk': jax.random.normal(ks[1], (D, D), dtype=jnp.float32) * scale, 'bk': jax.random.normal(ks[2], (D,), dtype=jnp.float32) * scale, 'Wv': jax.random.normal(ks[3], (D, D), dtype=jnp.float32) * scale, 'bv': jax.random.normal(ks[4], (D,), dtype=jnp.float32) * scale, 'Wq': jax.random.normal(ks[5], (D, D), dtype=jnp.float32) * scale, 'bq': jax.random.normal(ks[6], (D,), dtype=jnp.float32) * scale}
    _L0_attn_all = _L0_attn_setup()
    _L0_attn_in = {k: v for k, v in _L0_attn_all.items() if k in ('Wk', 'bk', 'Wv', 'bv', 'Wq', 'bq')}
    del _L0_attn_all

    def _L0_xattn_setup():
        import jax, jax.numpy as jnp
        import numpy as np
        import math
        NUM_HEADS = 16
        KEY_DIM = 64
        MODEL_DIM = 256
        NEG_INF = -1000000000.0

        def _get_slopes(n):

            def pow2_slopes(n):
                start = 2 ** (-2 ** (-(math.log2(n) - 3)))
                return [start * start ** i for i in range(n)]
            if math.log2(n).is_integer():
                s = pow2_slopes(n)
            else:
                c = 2 ** math.floor(math.log2(n))
                s = pow2_slopes(c) + pow2_slopes(2 * c)[0::2][:n - c]
            return jnp.asarray(s, dtype=jnp.float32)
        key = jax.random.key(seed)
        ks = jax.random.split(key, 11)
        B, S, D = (4, 512, MODEL_DIM)
        P = NUM_HEADS * KEY_DIM
        sd = 1.0 / math.sqrt(D)
        return {'query': jax.random.normal(ks[0], (B, S, D), jnp.float32), 'key': jax.random.normal(ks[1], (B, S, D), jnp.float32), 'value': jax.random.normal(ks[2], (B, S, D), jnp.float32), 'Wq': jax.random.normal(ks[3], (D, P), jnp.float32) * sd, 'bq': jnp.zeros((P,), jnp.float32), 'Wk': jax.random.normal(ks[4], (D, P), jnp.float32) * sd, 'bk': jnp.zeros((P,), jnp.float32), 'Wv': jax.random.normal(ks[5], (D, P), jnp.float32) * sd, 'bv': jnp.zeros((P,), jnp.float32), 'Wo': jax.random.normal(ks[6], (P, D), jnp.float32) * (1.0 / math.sqrt(P)), 'bo': jnp.zeros((D,), jnp.float32)}
    _L0_xattn_all = _L0_xattn_setup()
    _L0_xattn_in = {k: v for k, v in _L0_xattn_all.items() if k in ('Wq', 'bq', 'Wk', 'bk', 'Wv', 'bv', 'Wo', 'bo')}
    del _L0_xattn_all

    def _L0_ffn_setup():
        import jax, jax.numpy as jnp
        import numpy as np
        D_MODEL = 256
        D1, D2 = (32, 32)
        F1, F2 = (64, 64)
        E = 64
        TOP_K = 2

        def kmoe(x_flat, W_router, A, B, scale, bias, d_in1, d_in2, d_out1, d_out2, top_k):
            logits = x_flat @ W_router.T
            vals, idx = jax.lax.top_k(logits, top_k)
            probs = jax.nn.softmax(vals, axis=-1)
            xs = x_flat.reshape(-1, d_in1, d_in2)
            Ag = A[idx]
            Bg = B[idx]
            Y = jnp.einsum('nkoi,nij,nkpj->nkop', Ag, xs, Bg)
            out = jnp.einsum('nkop,nk->nop', Y, probs).reshape(-1, d_out1 * d_out2)
            return out * scale + bias
        key = jax.random.key(seed)
        ks = jax.random.split(key, 12)
        s = 0.02
        return {'x': jax.random.normal(ks[0], (4, 512, D_MODEL), dtype=jnp.float32), 'W_up': jax.random.normal(ks[1], (E, D1 * D2), dtype=jnp.float32) * s, 'A_up': jax.random.normal(ks[2], (E, F1, D1), dtype=jnp.float32) * s, 'B_up': jax.random.normal(ks[3], (E, F2, D2), dtype=jnp.float32) * s, 'scale_up': jnp.ones((1,), dtype=jnp.float32), 'bias_up': jnp.zeros((F1 * F2,), dtype=jnp.float32), 'W_down': jax.random.normal(ks[4], (E, F1 * F2), dtype=jnp.float32) * s, 'A_down': jax.random.normal(ks[5], (E, D1, F1), dtype=jnp.float32) * s, 'B_down': jax.random.normal(ks[6], (E, D2, F2), dtype=jnp.float32) * s, 'scale_down': jnp.ones((1,), dtype=jnp.float32), 'bias_down': jnp.zeros((D1 * D2,), dtype=jnp.float32)}
    _L0_ffn_all = _L0_ffn_setup()
    _L0_ffn_in = {k: v for k, v in _L0_ffn_all.items() if k in ('W_up', 'A_up', 'B_up', 'scale_up', 'bias_up', 'W_down', 'A_down', 'B_down', 'scale_down', 'bias_down')}
    del _L0_ffn_all
    return {'x': x, 'ctx_1024': ctx_1024, 'L0_attn_Wk': _L0_attn_in['Wk'], 'L0_attn_bk': _L0_attn_in['bk'], 'L0_attn_Wv': _L0_attn_in['Wv'], 'L0_attn_bv': _L0_attn_in['bv'], 'L0_attn_Wq': _L0_attn_in['Wq'], 'L0_attn_bq': _L0_attn_in['bq'], 'L0_xattn_Wq': _L0_xattn_in['Wq'], 'L0_xattn_bq': _L0_xattn_in['bq'], 'L0_xattn_Wk': _L0_xattn_in['Wk'], 'L0_xattn_bk': _L0_xattn_in['bk'], 'L0_xattn_Wv': _L0_xattn_in['Wv'], 'L0_xattn_bv': _L0_xattn_in['bv'], 'L0_xattn_Wo': _L0_xattn_in['Wo'], 'L0_xattn_bo': _L0_xattn_in['bo'], 'L0_ffn_W_up': _L0_ffn_in['W_up'], 'L0_ffn_A_up': _L0_ffn_in['A_up'], 'L0_ffn_B_up': _L0_ffn_in['B_up'], 'L0_ffn_scale_up': _L0_ffn_in['scale_up'], 'L0_ffn_bias_up': _L0_ffn_in['bias_up'], 'L0_ffn_W_down': _L0_ffn_in['W_down'], 'L0_ffn_A_down': _L0_ffn_in['A_down'], 'L0_ffn_B_down': _L0_ffn_in['B_down'], 'L0_ffn_scale_down': _L0_ffn_in['scale_down'], 'L0_ffn_bias_down': _L0_ffn_in['bias_down']}

def reference(x, ctx_1024, L0_attn_Wk, L0_attn_bk, L0_attn_Wv, L0_attn_bv, L0_attn_Wq, L0_attn_bq, L0_xattn_Wq, L0_xattn_bq, L0_xattn_Wk, L0_xattn_bk, L0_xattn_Wv, L0_xattn_bv, L0_xattn_Wo, L0_xattn_bo, L0_ffn_W_up, L0_ffn_A_up, L0_ffn_B_up, L0_ffn_scale_up, L0_ffn_bias_up, L0_ffn_W_down, L0_ffn_A_down, L0_ffn_B_down, L0_ffn_scale_down, L0_ffn_bias_down):
    import jax
    import jax.numpy as jnp

    def _L0_attn_ref(x, Wk, bk, Wv, bv, Wq, bq):
        import jax, jax.numpy as jnp
        import numpy as np
        B, S, D = (4, 1024, 256)
        k = jnp.fft.fft(x @ Wk.T + bk)
        v = jnp.fft.fft(x @ Wv.T + bv)
        q = jnp.fft.fft(x @ Wq.T + bq)
        inv_q = jnp.conj(q)
        kv = jnp.cumsum(k * v, axis=1)
        queried = kv * inv_q
        nrm = jnp.sqrt(jnp.sum(jnp.abs(queried) ** 2, axis=-1, keepdims=True))
        queried = queried / (1e-09 + nrm)
        d = x.shape[-1]
        return jnp.real(jnp.fft.ifft(queried)) / np.sqrt(d).astype(np.float32)

    def _L0_xattn_ref(query, key, value, Wq, bq, Wk, bk, Wv, bv, Wo, bo):
        import jax, jax.numpy as jnp
        import numpy as np
        import math
        NUM_HEADS = 16
        KEY_DIM = 64
        MODEL_DIM = 256
        NEG_INF = -1000000000.0

        def _get_slopes(n):

            def pow2_slopes(n):
                start = 2 ** (-2 ** (-(math.log2(n) - 3)))
                return [start * start ** i for i in range(n)]
            if math.log2(n).is_integer():
                s = pow2_slopes(n)
            else:
                c = 2 ** math.floor(math.log2(n))
                s = pow2_slopes(c) + pow2_slopes(2 * c)[0::2][:n - c]
            return jnp.asarray(s, dtype=jnp.float32)
        B, S, _ = query.shape
        H, Kd = (NUM_HEADS, KEY_DIM)

        def split_heads(x):
            return x.reshape(B, S, H, Kd).transpose(0, 2, 1, 3)
        q = split_heads(query @ Wq + bq)
        k = split_heads(key @ Wk + bk)
        v = split_heads(value @ Wv + bv)
        logits = jnp.einsum('bhqd,bhkd->bhqk', q, k) / jnp.sqrt(jnp.float32(Kd))
        i = jnp.arange(S)[:, None]
        j = jnp.arange(S)[None, :]
        causal = jnp.where(i >= j, 0.0, NEG_INF).astype(jnp.float32)
        rel = (i - j).astype(jnp.float32)
        slopes = _get_slopes(H)
        alibi = slopes[:, None, None] * rel
        logits = logits + causal[None, None, :, :] + alibi[None, :, :, :]
        weights = jax.nn.softmax(logits, axis=-1)
        attn = jnp.einsum('bhqk,bhkd->bhqd', weights, v)
        concat = attn.transpose(0, 2, 1, 3).reshape(B, S, H * Kd)
        return concat @ Wo + bo

    def _L0_ffn_ref(x, W_up, A_up, B_up, scale_up, bias_up, W_down, A_down, B_down, scale_down, bias_down):
        import jax, jax.numpy as jnp
        import numpy as np
        D_MODEL = 256
        D1, D2 = (32, 32)
        F1, F2 = (64, 64)
        E = 64
        TOP_K = 2

        def kmoe(x_flat, W_router, A, B, scale, bias, d_in1, d_in2, d_out1, d_out2, top_k):
            logits = x_flat @ W_router.T
            vals, idx = jax.lax.top_k(logits, top_k)
            probs = jax.nn.softmax(vals, axis=-1)
            xs = x_flat.reshape(-1, d_in1, d_in2)
            Ag = A[idx]
            Bg = B[idx]
            Y = jnp.einsum('nkoi,nij,nkpj->nkop', Ag, xs, Bg)
            out = jnp.einsum('nkop,nk->nop', Y, probs).reshape(-1, d_out1 * d_out2)
            return out * scale + bias
        orig_shape = x.shape
        x_flat = x.reshape(-1, D1 * D2)
        h = kmoe(x_flat, W_up, A_up, B_up, scale_up, bias_up, D1, D2, F1, F2, TOP_K)
        h = jax.nn.gelu(h, approximate=False)
        y = kmoe(h, W_down, A_down, B_down, scale_down, bias_down, F1, F2, D1, D2, TOP_K)
        return y.reshape(*orig_shape[:-1], D_MODEL)
    x = x + _L0_attn_ref(_layernorm(x, axis=-1), L0_attn_Wk, L0_attn_bk, L0_attn_Wv, L0_attn_bv, L0_attn_Wq, L0_attn_bq)
    x = x + _L0_xattn_ref(_layernorm(x, axis=-1), ctx_1024, ctx_1024, L0_xattn_Wq, L0_xattn_bq, L0_xattn_Wk, L0_xattn_bk, L0_xattn_Wv, L0_xattn_bv, L0_xattn_Wo, L0_xattn_bo)
    x = x + _L0_ffn_ref(_layernorm(x, axis=-1), L0_ffn_W_up, L0_ffn_A_up, L0_ffn_B_up, L0_ffn_scale_up, L0_ffn_bias_up, L0_ffn_W_down, L0_ffn_A_down, L0_ffn_B_down, L0_ffn_scale_down, L0_ffn_bias_down)
    return x

_drawn_inputs = setup_inputs


def setup_inputs(seed=0):
    import zlib

    import numpy as np

    out = dict(_drawn_inputs(seed))
    spreads = {'L0_xattn_bq': (0.0, 0.321),
     'L0_xattn_bk': (0.0, 0.8),
     'L0_xattn_bv': (0.0, 0.1),
     'L0_xattn_bo': (0.0, 0.1),
     'L0_ffn_bias_up': (0.0, 0.8),
     'L0_ffn_bias_down': (0.0, 0.1)}
    factors = {'L0_attn_Wk': 8.0,
     'L0_attn_bk': 8.0,
     'L0_attn_Wv': 8.0,
     'L0_attn_bv': 8.0,
     'L0_attn_Wq': 8.0,
     'L0_attn_bq': 8.0,
     'L0_ffn_W_up': 8.0,
     'L0_ffn_A_up': 8.0,
     'L0_ffn_B_up': 8.0,
     'L0_ffn_W_down': 8.0,
     'L0_ffn_A_down': 8.0,
     'L0_ffn_B_down': 8.0}
    for name, (base, spread) in spreads.items():
        noise = np.random.default_rng([zlib.crc32(name.encode()), seed]).standard_normal(out[name].shape)
        drawn = base * np.exp(spread * noise) if base else spread * noise
        out[name] = jnp.asarray(drawn.astype(out[name].dtype))
    for name, factor in factors.items():
        out[name] = (out[name] * factor).astype(out[name].dtype)
    return out
```

```python
import math
from contextlib import ExitStack

import numpy as np

import concourse.bass as bass
from concourse import mybir

F32 = mybir.dt.float32
I32 = mybir.dt.int32
U32 = mybir.dt.uint32
ALU = mybir.AluOpType
ACT = mybir.ActivationFunctionType

P = 128
BATCH, SEQ, DIM = 16, 256, 256
RT = SEQ // P
CT = DIM // P
HEADS, KEY = 16, 64
PAIRS = HEADS // 2
EXPERTS, TOPK = 64, 2
TOKENS = SEQ * DIM // 1024
D1, F1 = 32, 64
UP_TOK = P // D1
UP_GROUPS = TOKENS // UP_TOK
DN_TOK = 8
DN_GROUPS = TOKENS // DN_TOK
GROUPS = UP_GROUPS + DN_GROUPS
LN_EPS = 1e-5
BIG = 1.0e9
TOP = 3.0e38


def at(b, per_batch, k):
    return b * per_batch + k


def hold(eng, passed, sem, value):
    eng.wait_ge(sem, value)
    eng.sem_inc(passed, 1)


def spread(ap, axis, n):
    wide = ap.unsqueeze(axis)
    shape = list(wide.shape)
    shape[axis] = n
    return wide.to_broadcast(shape)


def decoder_layer(nc, t, out):
    ctx = ExitStack()
    with ctx:
        def sb(name, shape, dt=F32):
            return ctx.enter_context(nc.sbuf_tensor(name, shape, dt))

        def sem(name):
            return ctx.enter_context(nc.semaphore(name))

        ident = sb("ident", [P, P])
        ones = sb("ones", [F1, P])
        wf = sb("wf", [P, CT, 3, 256])
        bf = sb("bf", [P, 2, 4])
        idft = sb("idft", [P, 2, DIM])
        bin_weight = sb("bin_weight", [P, 1])
        wq = sb("wq", [P, CT, HEADS * KEY])
        wk = sb("wk", [P, CT, HEADS * KEY])
        wv = sb("wv", [P, CT, HEADS * KEY])
        wo = sb("wo", [P, PAIRS, DIM])
        bq = sb("bq", [P, PAIRS])
        bq_neg = sb("bq_neg", [P, PAIRS])
        bk = sb("bk", [P, PAIRS])
        bv = sb("bv", [P, PAIRS])
        out_bias = sb("out_bias", [P, DIM])
        neg_bias = sb("neg_bias", [P, HEADS, 2 * P])
        a_up = sb("a_up", [P, EXPERTS * F1])
        b_up = sb("b_up", [D1, EXPERTS * F1])
        a_dn = sb("a_dn", [P, EXPERTS * D1])
        b_dn = sb("b_dn", [F1, EXPERTS * D1])
        r_up = sb("r_up", [P, 2 * UP_TOK, EXPERTS])
        r_dn = sb("r_dn", [P, F1 // 2, EXPERTS])
        bias_up = sb("bias_up", [F1, F1])
        bias_dn = sb("bias_dn", [D1, D1])
        scale_up = sb("scale_up", [F1, 1])
        scale_dn = sb("scale_dn", [D1, 1])
        own_up = sb("own_up", [P, UP_TOK * TOPK])
        own_dn = sb("own_dn", [P, 2 * TOPK])

        x = sb("x", [P, RT, DIM])
        x1 = sb("x1", [P, RT, DIM])
        x2 = sb("x2", [P, RT, DIM])
        ctxT = sb("ctxT", [P, CT, SEQ])
        xn = sb("xn", [P, RT, DIM])
        xnT = sb("xnT", [P, CT, SEQ])
        xn3 = sb("xn3", [P, RT, DIM])
        xn3T = sb("xn3T", [P, CT, SEQ])
        stats = sb("stats", [P, 3, RT, 6])
        moments = sb("moments", [P, 3, RT, 2])
        var_eps = sb("var_eps", [P, 3, RT])
        rstd = sb("rstd", [P, 3, RT])
        root, inv_root = sb("root", [P, RT]), sb("inv_root", [P, RT])
        shared = sb("shared", [P, 6, 512])
        kF, vF, qF, prodA, prodB, KV = (shared[:, i, :] for i in range(6))
        Q, Qsq = kF, vF
        probs = [shared[:, i, 0:384] for i in (0, 1)]
        probsT = [shared[:, i, 0:384] for i in (2, 3)]
        pair = [shared[:, 4, i * 256:(i + 1) * 256].rearrange("p (t d) -> p t d", t=RT) for i in (0, 1)]
        fpower = sb("fpower", [P, RT])
        fnorm = sb("fnorm", [P, RT])
        fscale = sb("fscale", [P, RT])
        qT = sb("qT", [P, PAIRS, SEQ])
        kT = sb("kT", [P, PAIRS, SEQ])
        vals = sb("vals", [P, RT, HEADS, KEY + 1])
        neg_max = sb("neg_max", [P, 2, RT])
        rsum = sb("rsum", [P, 2, 2, RT])
        h = sb("h", [P, TOKENS * F1])
        pre = [sb(f"pre{i}", [F1, UP_TOK * F1]) for i in (0, 1)]
        small = sb("small", [D1, TOKENS * D1])
        yT = sb("yT", [P, CT, SEQ])
        W = [sb(f"W{i}", [P, 512]) for i in (0, 1)]
        top_val = sb("top_val", [F1, 8])
        top_idx = sb("top_idx", [F1, 8], U32)
        gap = sb("gap", [F1, 1])
        egap = sb("egap", [F1, 1])
        den = sb("den", [F1, 1])
        prob = sb("prob", [F1, TOPK])
        place = sb("place", [F1, TOPK])
        route_diag = sb("route_diag", [F1, 2 * TOKENS * TOPK])
        pm = sb("pm", [P, TOKENS * TOPK])
        offsets = sb("offsets", [1, TOKENS * TOPK], I32)

        wnat = h[:, 0:1536].rearrange("p (i j c) -> p i j c", i=3, j=2)
        dft = h[:, 1536:2048].rearrange("p (j f) -> p j f", j=2)
        bv_wide = h[:, 2048:3072].rearrange("p (m n) -> p m n", m=PAIRS)
        bnat = h[:, 3072:3078].rearrange("p (j i) -> p j i", j=2)
        bo_row = h[0:1, 3328:3584]

        def bank(name):
            return ctx.enter_context(nc.psum_tensor(name, [P, 512], F32))

        TR, S0, S1, PT, O, FA, FB, G = (bank(n) for n in ("TR", "S0", "S1", "PT", "O", "FA", "FB", "G"))
        S, F, X = [S0, S1], [FA, FB], [O, TR]
        k_banks = v_banks = q_banks = [S0, S1, PT, O]

        fourier_tables, attn_tables, ffn_tables = sem("fourier_tables"), sem("attn_tables"), sem("ffn_tables")
        folded, folded_kept, bv_spread, bias_made, vals_ones, exponents = (
            sem("folded"), sem("folded_kept"), sem("bv_spread"), sem("bias_made"), sem("vals_ones"), sem("exponents"))
        x_loaded, ctx_loaded, out_stored = sem("x_loaded"), sem("ctx_loaded"), sem("out_stored")
        ln_stats = [sem(f"ln{i}_stats") for i in (1, 2, 3)]
        ln_moments = [sem(f"ln{i}_moments") for i in (1, 2, 3)]
        ln_rstd = [sem(f"ln{i}_rstd") for i in (1, 2, 3)]
        ln_done = [sem(f"ln{i}_done") for i in (1, 2, 3)]
        xn_turned, xnT_ready = sem("xn_turned"), sem("xnT_ready")
        proj_done = sem("proj_done")
        proj_kept = sem("proj_kept")
        straight, crossed, lane_fixed = sem("straight"), sem("crossed"), sem("lane_fixed")
        summed, Q_ready, Qsq_ready = sem("summed"), sem("Q_ready"), sem("Qsq_ready")
        inverse_done, fpower_kept = sem("inverse_done"), sem("fpower_kept")
        fnorm_step, fscale_ready = sem("fnorm_step"), sem("fscale_ready")
        x1_done, x1_biased, x2_done = sem("x1_done"), sem("x1_biased"), sem("x2_done")
        scores_done, scores_masked, probs_ready = sem("scores_done"), sem("scores_masked"), sem("probs_ready")
        probs_turned, probsT_act, probsT_dve = sem("probs_turned"), sem("probsT_act"), sem("probsT_dve")
        pv_done, rsum_ready, pair_normed = sem("pv_done"), sem("rsum_ready"), sem("pair_normed")
        pair_turned, pair_kept, wo_done = sem("pair_turned"), sem("pair_kept"), sem("wo_done")
        xn3_turned, xn3T_ready = sem("xn3_turned"), sem("xn3T_ready")
        small_act, small_dve = sem("small_act"), sem("small_dve")
        logits_done, top_found, gap_exp = sem("logits_done"), sem("top_found"), sem("gap_exp")
        gap_ready, route_step, route_ready = sem("gap_ready"), sem("route_step"), sem("route_ready")
        route_spread, pm_ready, offsets_ready = sem("route_spread"), sem("pm_ready"), sem("offsets_ready")
        first_done, W_ready, second_done = sem("first_done"), sem("W_ready"), sem("second_done")
        hidden_in, h_ready, y_kept = sem("hidden_in"), sem("h_ready"), sem("y_kept")
        yT_act, yT_dve, y_turned, out_ready = sem("yT_act"), sem("yT_dve"), sem("y_turned"), sem("out_ready")

        result_free = sem("result_free")
        passed = sem("passed")
        FOURIER_LOADS = 6
        ATTN_LOADS = 10
        FFN_LOADS = 13

        block = ctx.enter_context(nc.Block())

        def both_halves(run, eng):
            run(0, None)
            with eng.Fori(0, BATCH - 1) as c:
                run(c + 1, c)
            run(None, BATCH - 1)

        ORDER = ([("k_proj", None), ("ln1", None), ("ln3", None), ("f_proj", None), ("logits_up", None),
                  ("v_proj", None), ("route_up", None)]
                 + [("up", g) for g in range(0, 4)] + [("fourier", None)]
                 + [("up", g) for g in range(4, 10)] + [("inverse", None)]
                 + [("up", g) for g in range(10, 14)] + [("ln2", None)]
                 + [("up", g) for g in range(14, UP_GROUPS + 1)]
                 + [("logits_dn", None), ("q_proj", None), ("route_dn", None)])
        for i in range(HEADS + 3):
            ORDER.append(("head", i))
            if i % 2 == 1 and i // 2 <= DN_GROUPS:
                ORDER.append(("down", i // 2))
        ORDER += [("final", None), ("wo", None)]
        ATTN_STEPS = {"k_proj", "ln1", "f_proj", "v_proj", "fourier", "inverse", "ln2", "q_proj", "head", "wo"}

        def go(steps, b, c):
            for name, n in ORDER:
                which = b if name in ATTN_STEPS else c
                if which is None or name not in steps:
                    continue
                if n is None:
                    steps[name](which)
                else:
                    steps[name](which, n)

        @block.sync
        def _(sp):
            for dst, src in ((wnat[:, 0], t["Wk"]), (wnat[:, 1], t["Wv"]), (wnat[:, 2], t["Wq"]), (dft, t["dft"])):
                sp.dma_start(dst, src.rearrange("(j p) c -> p j c", p=P)).then_inc(fourier_tables, 16)
            sp.dma_start(bnat, t["b_fourier"]).then_inc(fourier_tables, 16)
            sp.dma_start(ident[:, :], t["ident"]).then_inc(fourier_tables, 16)

            def load(b):
                if not isinstance(b, int) or b > 0:
                    sp.wait_ge(x1_done, at(b, 2, 0))
                    sp.wait_ge(proj_done, at(b, 15, -4))
                sp.dma_start(x[:, :, :], t["x"][b].rearrange("(t p) c -> p t c", p=P)).then_inc(x_loaded, 16)
                sp.dma_start(ctxT[:, :, :], t["ctxT"][b].rearrange("(t p) s -> p t s", p=P)).then_inc(ctx_loaded, 16)

            def store(c):
                sp.wait_ge(out_ready, at(c, 1, 1))
                sp.dma_start(out[c].rearrange("(t p) c -> p t c", p=P), xn3[:, :, :]).then_inc(out_stored, 16)
                sp.wait_ge(out_stored, at(c, 16, 16))
                sp.sem_inc(result_free, 1)

            load(0)
            sp.sem_inc(result_free, 1)
            sp.dma_start(idft[:, :, :], t["idft"].rearrange("(j p) c -> p j c", p=P)).then_inc(attn_tables, 16)
            sp.dma_start(bin_weight[:, :], t["bin_weight"]).then_inc(attn_tables, 16)
            for dst, name in ((wk, "xWk"), (wv, "xWv"), (wq, "xWq"), (wo, "xWo")):
                sp.dma_start(dst[:, :, :], t[name].rearrange("(j p) c -> p j c", p=P)).then_inc(attn_tables, 16)
            for dst, name in ((bq, "xbq"), (bk, "xbk"), (bv, "xbv")):
                sp.dma_start(dst[:, :], t[name]).then_inc(attn_tables, 16)
            sp.dma_start(bo_row, t["xbo"]).then_inc(attn_tables, 16)
            sp.dma_start(neg_bias[:, :, :], t["neg_bias"]).then_inc(ffn_tables, 16)
            for dst, name in ((r_up, "r_up"), (r_dn, "r_dn")):
                sp.dma_start(dst[:, :, :], t[name]).then_inc(ffn_tables, 16)
            for dst, name in ((b_up, "b_up"), (a_up, "a_up"), (b_dn, "b_dn"), (a_dn, "a_dn"), (bias_up, "bias_up"),
                              (bias_dn, "bias_dn"), (own_up, "own_up"), (own_dn, "own_dn")):
                sp.dma_start(dst[:, :], t[name]).then_inc(ffn_tables, 16)
            sp.dma_start(scale_up[:, :], t["scale_up"].to_broadcast([F1, 1])).then_inc(ffn_tables, 16)
            sp.dma_start(scale_dn[:, :], t["scale_dn"].to_broadcast([D1, 1])).then_inc(ffn_tables, 16)

            load(1)
            with sp.Fori(0, BATCH - 2) as c:
                load(c + 2)
                store(c)
            store(BATCH - 2)
            store(BATCH - 1)

        @block.gpsimd
        def _(pool):
            pool.memset(vals[:, :, :, KEY:KEY + 1], 1.0).then_inc(vals_ones, 1)
            pool.memset(ones[:, :], 1.0).then_inc(vals_ones, 1)
            pool.memset(root[:, :], 0.5).then_inc(exponents, 1)
            pool.memset(inv_root[:, :], -0.5).then_inc(exponents, 1)
            pool.wait_ge(exponents, 2)

            def deviation(b, k):
                hold(pool, passed, ln_moments[k], at(b, 2, 2))
                pool.tensor_scalar(var_eps[:, k, :], moments[:, k, :, 1], LN_EPS, None, ALU.add).then_inc(ln_rstd[k], 1)
                pool.wait_ge(ln_rstd[k], at(b, 2, 1))
                pool.tensor_tensor(rstd[:, k, :], var_eps[:, k, :], inv_root[:, :], ALU.pow).then_inc(ln_rstd[k], 1)

            def inverse(b):
                pool.wait_ge(fpower_kept, at(b, 1, 1))
                pool.tensor_tensor(fnorm[:, :], fpower[:, :], root[:, :], ALU.pow).then_inc(fnorm_step, 1)
                hold(pool, passed, fnorm_step, at(b, 2, 1))
                pool.tensor_scalar(fnorm[:, :], fnorm[:, :], 1e-9, None, ALU.add).then_inc(fnorm_step, 1)

            def cross(b, k, left, left_sem, left_n, right):
                pool.wait_ge(left_sem, left_n)
                pool.wait_ge(proj_kept, at(b, 26, 12 + 2 * k))
                pool.tensor_tensor(prodB[:, 0:256], left[:, 0:256], right[:, 256:512], ALU.mult).then_inc(crossed, 1)
                pool.tensor_tensor(prodB[:, 256:512], left[:, 256:512], right[:, 0:256], ALU.mult).then_inc(crossed, 1)
                pool.wait_ge(straight, at(b, 2, k + 1))
                hold(pool, passed, crossed, at(b, 4, 2 * k + 2))
                to, zero = (0, 256) if k == 0 else (256, 0)
                pool.tensor_copy(prodB[0:1, to:to + 256], prodA[0:1, 256:512]).then_inc(lane_fixed, 1)
                pool.memset(prodB[0:1, zero:zero + 256], 0.0).then_inc(lane_fixed, 1)
                hold(pool, passed, lane_fixed, at(b, 6, 3 * k + 2))
                pool.memset(prodA[0:1, 256:512], 0.0).then_inc(lane_fixed, 1)

            def fourier(b):
                cross(b, 0, kF, proj_kept, at(b, 26, 12), vF)
                cross(b, 1, KV, summed, at(b, 2, 2), qF)

            def ln2(b):
                deviation(b, 1)
                pool.wait_ge(ln_done[1], at(b, 2, 2))
                pool.wait_ge(bias_made, 1)
                pool.tensor_tensor(x1[:, :, :], x1[:, :, :], spread(out_bias[:, :], 1, RT), ALU.add).then_inc(x1_biased, 1)

            steps = {"ln1": lambda b: deviation(b, 0), "fourier": fourier, "inverse": inverse, "ln2": ln2,
                     "ln3": lambda c: deviation(c, 2)}
            both_halves(lambda b, c: go(steps, b, c), pool)

        @block.scalar
        def _(act):
            act.wait_ge(folded, 3)
            for i, s in enumerate((S0, S1, PT)):
                act.copy(wf[:, :, i, :], s[:, :].rearrange("p (j f) -> p j f", j=CT)).then_inc(folded_kept, 1)
            act.wait_ge(folded, 4)
            act.copy(bf[:, :, 0:3], TR[:, 0:8].rearrange("p (j i) -> p j i", j=2)[:, :, 0:3]).then_inc(folded_kept, 1)
            act.wait_ge(attn_tables, 16 * ATTN_LOADS)
            act.mul(bq_neg[:, :], bq[:, :], -1.0 / math.sqrt(KEY)).then_inc(folded_kept, 1)
            act.wait_ge(folded, 5)
            act.copy(out_bias[:, :], O[:, 0:DIM]).then_inc(bias_made, 1)
            act.wait_ge(folded_kept, 5)

            def k_proj(b):
                for r in range(4):
                    act.wait_ge(proj_done, at(b, 15, r + 1))
                    for i in range(2):
                        m = 2 * r + i
                        act.activation(kT[:, m, :], k_banks[r][:, i * 256:(i + 1) * 256], ACT.Identity,
                                       bias=bk[:, m:m + 1]).then_inc(proj_kept, 1)

            def keep_xnT(b, k):
                act.wait_ge(xn_turned, at(b, 2, k))
                act.copy(xnT[:, :, :], TR[:, :].rearrange("p (c s) -> p c s", c=CT)).then_inc(xnT_ready, 1)

            def f_proj(b):
                for i, (dst, s) in enumerate(((kF, S0), (vF, S1), (qF, PT))):
                    act.wait_ge(proj_done, at(b, 15, 5 + i))
                    for half in range(2):
                        act.activation(dst[:, half * 256:(half + 1) * 256], s[:, half * 256:(half + 1) * 256],
                                       ACT.Identity, bias=bf[:, half, i:i + 1]).then_inc(proj_kept, 1)

            def v_proj(b):
                if isinstance(b, int):
                    act.wait_ge(vals_ones, 2)
                for r in range(4):
                    act.wait_ge(proj_done, at(b, 15, 8 + r))
                    act.copy(vals[:, r // 2, (r % 2) * 8:(r % 2) * 8 + 8, 0:KEY],
                             v_banks[r][:, :].rearrange("p (h d) -> p h d", d=KEY)).then_inc(proj_kept, 1)

            def inverse(b):
                act.wait_ge(Q_ready, at(b, 2, 2))
                act.activation(Qsq, Q, ACT.Square).then_inc(Qsq_ready, 1)

            def q_proj(b):
                for r in range(4):
                    act.wait_ge(proj_done, at(b, 15, 12 + r))
                    for i in range(2):
                        m = 2 * r + i
                        act.activation(qT[:, m, :], q_banks[r][:, i * 256:(i + 1) * 256], ACT.Identity,
                                       bias=bq_neg[:, m:m + 1], scale=-1.0 / math.sqrt(KEY)).then_inc(proj_kept, 1)

            def head(b, i):
                if i < HEADS:
                    act.wait_ge(scores_masked, at(b, 32, 2 * i + 2))
                    for rt, (lo, hi) in enumerate(((0, 128), (128, 384))):
                        act.activation(probs[i % 2][:, lo:hi], probs[i % 2][:, lo:hi], ACT.Exp,
                                       bias=neg_max[:, i % 2, rt:rt + 1], scale=-1.0).then_inc(probs_ready, 1)
                e = i - 1
                if 0 <= e < HEADS and e % 2 == 0:
                    act.wait_ge(probs_turned, at(b, 16, e + 1))
                    if e >= 2:
                        act.wait_ge(pv_done, at(b, 16, e - 1))
                    act.copy(probsT[e % 2], PT[:, 0:384]).then_inc(probsT_act, 1)
                if i >= 4 and i % 2 == 0:
                    m = (i - 4) // 2
                    act.wait_ge(pair_turned, at(b, 8, m + 1))
                    act.copy(qT[:, m, :], X[m % 2][:, 0:256]).then_inc(pair_kept, 1)

            def ln3(c):
                act.wait_ge(xn3_turned, at(c, 1, 1))
                act.copy(xn3T[:, :, :], FA[:, :].rearrange("p (c s) -> p c s", c=CT)).then_inc(xn3T_ready, 1)
                act.wait_ge(xn3T_ready, at(c, 1, 1))
                for il in range(4):
                    dst = small[:, :].rearrange("j (s i) -> j s i", i=8)[:, :, il]
                    act.copy(dst, xn3T[il * D1:(il + 1) * D1, 0, :]).then_inc(small_act, 1)

            def route_exp(c, layer):
                act.wait_ge(gap_ready, at(c, 2, layer + 1))
                act.activation(egap[:, :], gap[:, :], ACT.Exp).then_inc(gap_exp, 1)

            def up(c, g):
                if g == 0:
                    return
                g -= 1
                act.wait_ge(hidden_in, at(c, 16, g + 1))
                cols = slice(g * UP_TOK * F1, (g + 1) * UP_TOK * F1)
                above = h[F1:P, cols].rearrange("p (n q two) -> p n q two", n=UP_TOK, two=2)[:, :, :, 0]
                odd = pre[g % 2][:, :].rearrange("p (n q two) -> p n q two", n=UP_TOK, two=2)[:, :, :, 1]
                act.activation(h[0:F1, cols], pre[g % 2][:, :], ACT.Gelu).then_inc(h_ready, 1)
                act.activation(above, odd, ACT.Gelu).then_inc(h_ready, 1)

            def final(c):
                act.wait_ge(y_kept, at(c, 8, DN_GROUPS))
                parts = small[:, :].rearrange("p (s c i) -> p c s i", c=CT, i=4)
                for il in range(2):
                    act.copy(yT[il * D1:(il + 1) * D1, :, :], parts[:, :, :, il]).then_inc(yT_act, 1)

            steps = {"k_proj": k_proj, "ln1": lambda b: keep_xnT(b, 1), "f_proj": f_proj, "v_proj": v_proj,
                     "inverse": inverse, "ln2": lambda b: keep_xnT(b, 2), "q_proj": q_proj, "head": head,
                     "ln3": ln3, "route_up": lambda c: route_exp(c, 0), "up": up,
                     "route_dn": lambda c: route_exp(c, 1), "final": final}
            both_halves(lambda b, c: go(steps, b, c), act)

        @block.tensor
        def _(pe):
            pe.wait_ge(fourier_tables, 16 * FOURIER_LOADS)
            for i, s in enumerate((S0, S1, PT)):
                for ct in range(CT):
                    for j in range(2):
                        mm = pe.matmul(s[:, ct * 256:(ct + 1) * 256], wnat[:, i, j, ct * P:(ct + 1) * P],
                                       dft[:, j, :], start=(j == 0), stop=(j == 1))
                mm.then_inc(folded, 1)
            for half in range(2):
                for j in range(2):
                    mm = pe.matmul(TR[:, 4 * half:4 * half + 3], dft[:, j, half * P:(half + 1) * P],
                                   bnat[:, j, :], start=(j == 0), stop=(j == 1))
            mm.then_inc(folded, 1)
            pe.wait_ge(attn_tables, 16 * ATTN_LOADS)
            pe.wait_ge(bv_spread, 1)
            pe.wait_ge(vals_ones, 2)
            for m in range(PAIRS):
                pe.matmul(O[:, 0:DIM], bv_wide[:, m, :], wo[:, m, :], start=(m == 0), stop=False)
            pe.matmul(O[:, 0:DIM], ones[0:1, :], bo_row, start=False, stop=True).then_inc(folded, 1)
            pe.wait_ge(folded_kept, 5)
            pe.wait_ge(bias_made, 1)

            def k_proj(b):
                pe.wait_ge(ctx_loaded, at(b, 16, 16))
                pe.wait_ge(scores_masked, at(b, 32, 0))
                pe.wait_ge(probsT_act, at(b, 8, 0))
                pe.wait_ge(probsT_dve, at(b, 8, 0))
                pe.wait_ge(x2_done, at(b, 1, 0))
                for r in range(4):
                    for i in range(2):
                        m = 2 * r + i
                        for ct in range(CT):
                            mm = pe.matmul(k_banks[r][:, i * 256:(i + 1) * 256], wk[:, ct, m * P:(m + 1) * P],
                                           ctxT[:, ct, :], start=(ct == 0), stop=(ct == CT - 1))
                    mm.then_inc(proj_done, 1)

            def turn(b, k):
                pe.wait_ge(ln_done[k - 1], at(b, 2, 2))
                if k == 1:
                    pe.wait_ge(pair_kept, at(b, 8, 0))
                else:
                    pe.wait_ge(x1_done, at(b, 2, 2))
                for ct in range(CT):
                    for rt in range(RT):
                        mm = pe.transpose(TR[:, ct * 256 + rt * P:ct * 256 + (rt + 1) * P],
                                          xn[:, rt, ct * P:(ct + 1) * P], ident[:, :])
                mm.then_inc(xn_turned, 1)

            def f_proj(b):
                pe.wait_ge(xnT_ready, at(b, 2, 1))
                for i, s in enumerate((S0, S1, PT)):
                    pe.wait_ge(proj_kept, at(b, 26, 2 * i + 2))
                    for half in range(2):
                        for ct in range(CT):
                            mm = pe.matmul(s[:, half * 256:(half + 1) * 256], wf[:, ct, i, half * P:(half + 1) * P],
                                           xnT[:, ct, :], start=(ct == 0), stop=(ct == CT - 1))
                    mm.then_inc(proj_done, 1)

            def v_proj(b):
                for r in range(4):
                    pe.wait_ge(proj_kept, at(b, 26, 10 + 2 * r if r < 3 else 8))
                    for ct in range(CT):
                        mm = pe.matmul(v_banks[r][:, :], ctxT[:, ct, (r // 2) * P:(r // 2 + 1) * P],
                                       wv[:, ct, (r % 2) * 512:(r % 2 + 1) * 512], start=(ct == 0), stop=(ct == CT - 1))
                    mm.then_inc(proj_done, 1)

            def inverse(b):
                pe.wait_ge(Q_ready, at(b, 2, 2))
                pe.wait_ge(proj_kept, at(b, 26, 18))
                for rt in range(RT):
                    for half in range(2):
                        pe.matmul(O[:, rt * 256:(rt + 1) * 256], Q[:, half * 256 + rt * P:half * 256 + (rt + 1) * P],
                                  idft[:, half, :], start=(half == 0), stop=(half == 1))
                pe.wait_ge(Qsq_ready, at(b, 1, 1))
                for rt in range(RT):
                    for half in range(2):
                        mm = pe.matmul(TR[:, rt:rt + 1], Qsq[:, half * 256 + rt * P:half * 256 + (rt + 1) * P],
                                       bin_weight[:, :], start=(half == 0), stop=(half == 1))
                mm.then_inc(inverse_done, 1)

            def q_proj(b):
                pe.wait_ge(xnT_ready, at(b, 2, 2))
                for r in range(4):
                    if r == 3:
                        pe.wait_ge(x1_done, at(b, 2, 2))
                    else:
                        pe.wait_ge(proj_kept, at(b, 26, 15 + r))
                    for i in range(2):
                        m = 2 * r + i
                        for ct in range(CT):
                            mm = pe.matmul(q_banks[r][:, i * 256:(i + 1) * 256], wq[:, ct, m * P:(m + 1) * P],
                                           xnT[:, ct, :], start=(ct == 0), stop=(ct == CT - 1))
                    mm.then_inc(proj_done, 1)

            def head(b, i):
                if i < HEADS:
                    m, lo = i // 2, (i % 2) * KEY
                    if i == 0:
                        pe.wait_ge(proj_kept, at(b, 26, 26))
                    elif i >= 2:
                        pe.wait_ge(scores_masked, at(b, 32, 2 * i - 2))
                    pe.matmul(S[i % 2][:, 0:P], qT[lo:lo + KEY, m, 0:P], kT[lo:lo + KEY, m, 0:P], start=True, stop=True)
                    pe.matmul(S[i % 2][:, P:3 * P], qT[lo:lo + KEY, m, P:2 * P], kT[lo:lo + KEY, m, :],
                              start=True, stop=True).then_inc(scores_done, 1)
                e = i - 1
                if 0 <= e < HEADS:
                    pe.wait_ge(probs_ready, at(b, 32, 2 * e + 2))
                    if e >= 1:
                        if (e - 1) % 2 == 0:
                            pe.wait_ge(probsT_act, at(b, 8, (e - 1) // 2 + 1))
                        else:
                            pe.wait_ge(probsT_dve, at(b, 8, (e - 1) // 2 + 1))
                    for j in range(3):
                        mm = pe.transpose(PT[:, j * P:(j + 1) * P], probs[e % 2][:, j * P:(j + 1) * P], ident[:, :])
                    mm.then_inc(probs_turned, 1)
                e = i - 2
                if 0 <= e < HEADS:
                    if e % 2 == 0:
                        pe.wait_ge(probsT_act, at(b, 8, e // 2 + 1))
                    else:
                        pe.wait_ge(probsT_dve, at(b, 8, e // 2 + 1))
                    m = e // 2
                    if e % 2 == 0 and m >= 2:
                        pe.wait_ge(pair_kept, at(b, 8, m - 1))
                    to, o = X[m % 2], (e % 2) * RT * (KEY + 1)
                    p = probsT[e % 2]
                    pe.matmul(to[:, o:o + KEY + 1], p[:, 0:P], vals[:, 0, e, :], start=True, stop=True)
                    o += KEY + 1
                    pe.matmul(to[:, o:o + KEY + 1], p[:, P:2 * P], vals[:, 0, e, :], start=True, stop=False)
                    pe.matmul(to[:, o:o + KEY + 1], p[:, 2 * P:3 * P], vals[:, 1, e, :], start=False, stop=True)\
                      .then_inc(pv_done, 1)
                if i >= 4 and i % 2 == 0:
                    turn_pair(b, (i - 4) // 2)

            def turn_pair(b, m):
                pe.wait_ge(pair_normed, at(b, 8, m + 1))
                for rt in range(RT):
                    mm = pe.transpose(X[m % 2][:, rt * P:(rt + 1) * P], pair[m % 2][:, rt, :], ident[:, :])
                mm.then_inc(pair_turned, 1)

            def wo_proj(b):
                pe.wait_ge(pair_kept, at(b, 8, PAIRS))
                for rt in range(RT):
                    for m in range(PAIRS):
                        mm = pe.matmul(O[:, rt * 256:(rt + 1) * 256], qT[:, m, rt * P:(rt + 1) * P], wo[:, m, :],
                                       start=(m == 0), stop=(m == PAIRS - 1))
                mm.then_inc(wo_done, 1)

            def ln3(c):
                pe.wait_ge(ln_done[2], at(c, 2, 2))
                for ct in range(CT):
                    for rt in range(RT):
                        mm = pe.transpose(FA[:, ct * 256 + rt * P:ct * 256 + (rt + 1) * P],
                                          xn3[:, rt, ct * P:(ct + 1) * P], ident[:, :])
                mm.then_inc(xn3_turned, 1)

            def logits_up(c):
                pe.wait_ge(xn3T_ready, at(c, 1, 1))
                pe.wait_ge(ffn_tables, 16 * FFN_LOADS)
                for r in range(UP_TOK):
                    for ct in range(CT):
                        n = r * CT + ct
                        rows = xn3T[:, ct, :].rearrange("p (n r) -> p r n", r=UP_TOK)[:, r, :]
                        mm = pe.matmul(G[0:F1, 0:EXPERTS], rows, r_up[:, n, :], start=(n == 0), stop=(n == 2 * UP_TOK - 1))
                mm.then_inc(logits_done, 1)

            def logits_dn(c):
                pe.wait_ge(h_ready, at(c, 32, 32))
                cols = h[:, :].rearrange("p (n q two) -> p two q n", n=TOKENS, two=2)
                for q in range(F1 // 2):
                    mm = pe.matmul(G[0:F1, 0:EXPERTS], cols[:, 0, q, :], r_dn[:, q, :], start=(q == 0), stop=(q == F1 // 2 - 1))
                mm.then_inc(logits_done, 1)

            def route(c, layer):
                pe.wait_ge(route_ready, at(c, 4, 2 * layer + 2))
                pe.matmul(G[:, 128:384], ones[0:F1, :], route_diag[:, :], start=True, stop=True).then_inc(route_spread, 1)

            def load_offsets(c, layer, first, n):
                if first == 0:
                    hold(pe, passed, offsets_ready, at(c, 2, layer + 1))
                return nc.values_load_multi_w_load_instructions(
                    offsets[0:1, first:first + n], engines=[mybir.EngineType.PE], min_val=0,
                    max_val=(EXPERTS - 1) * (F1 if layer == 0 else D1),
                    skip_runtime_bounds_check_because="an index of one of 64 logits times the table's step")[1]

            held = {}

            def up(c, g):
                if g < UP_GROUPS:
                    e = held[g % 2] = load_offsets(c, 0, g * 8, 8)
                    if g == 0:
                        pe.wait_ge(small_act, at(c, 4, 4))
                        pe.wait_ge(small_dve, at(c, 4, 4))
                    elif g >= 2:
                        pe.wait_ge(W_ready, at(c, GROUPS, g - 1))
                    for k in range(8):
                        mm = pe.matmul(F[g % 2][:, k * F1:(k + 1) * F1], small[:, g * P:(g + 1) * P],
                                       b_up[:, bass.ds(e[k], F1)], start=True, stop=True)
                    mm.then_inc(first_done, 1)
                if g >= 1:
                    g -= 1
                    e = held[g % 2]
                    pe.wait_ge(W_ready, at(c, GROUPS, g + 1))
                    if g >= 1:
                        pe.wait_ge(hidden_in, at(c, 16, g))
                    else:
                        pe.wait_ge(pm_ready, at(c, 2, 1))
                    for n in range(UP_TOK):
                        o = n * F1
                        for k in range(TOPK):
                            s = n * TOPK + k
                            mm = pe.matmul(G[0:F1, o:o + F1], W[g % 2][:, s * F1:(s + 1) * F1],
                                           a_up[:, bass.ds(e[s], F1)], start=(k == 0), stop=(k == TOPK - 1))
                    mm.then_inc(second_done, 1)

            def down(c, g):
                if g < DN_GROUPS:
                    e = held[g % 2] = load_offsets(c, 1, g * 16, 16)
                    if g >= 1:
                        pe.wait_ge(W_ready, at(c, GROUPS, UP_GROUPS + g - 1))
                    for k in range(16):
                        first = (g * DN_TOK + k // 4 * 2) * F1
                        mm = pe.matmul(F[g % 2][:, k * D1:(k + 1) * D1], h[0:F1, first:first + P],
                                       b_dn[:, bass.ds(e[k], D1)], start=True, stop=True)
                    mm.then_inc(first_done, 1)
                if g >= 1:
                    g -= 1
                    e = held[g % 2]
                    pe.wait_ge(W_ready, at(c, GROUPS, UP_GROUPS + g + 1))
                    if g >= 1:
                        pe.wait_ge(y_kept, at(c, 8, g))
                    else:
                        pe.wait_ge(pm_ready, at(c, 2, 2))
                    for n in range(DN_TOK):
                        o = n * D1
                        for k in range(TOPK):
                            s = n * TOPK + k
                            mm = pe.matmul(G[0:D1, o:o + D1], W[g % 2][:, s * D1:(s + 1) * D1],
                                           a_dn[:, bass.ds(e[s], D1)], start=(k == 0), stop=(k == TOPK - 1))
                    mm.then_inc(second_done, 1)

            def final(c):
                pe.wait_ge(yT_act, at(c, 2, 2))
                pe.wait_ge(yT_dve, at(c, 2, 2))
                for rt in range(RT):
                    for ct in range(CT):
                        mm = pe.transpose(FA[:, rt * 256 + ct * P:rt * 256 + (ct + 1) * P],
                                          yT[:, ct, rt * P:(rt + 1) * P], ident[:, :])
                mm.then_inc(y_turned, 1)

            steps = {"k_proj": k_proj, "ln1": lambda b: turn(b, 1), "f_proj": f_proj, "v_proj": v_proj,
                     "inverse": inverse, "ln2": lambda b: turn(b, 2), "q_proj": q_proj, "head": head, "wo": wo_proj,
                     "ln3": ln3, "logits_up": logits_up, "route_up": lambda c: route(c, 0), "up": up,
                     "logits_dn": logits_dn, "route_dn": lambda c: route(c, 1), "down": down, "final": final}
            both_halves(lambda b, c: go(steps, b, c), pe)

        @block.vector
        def _(dve):
            dve.wait_ge(attn_tables, 16 * ATTN_LOADS)
            dve.tensor_copy(bv_wide, spread(bv[:, :], 2, P)).then_inc(bv_spread, 1)

            def layernorm(b, k, src, dst):
                for rt in range(RT):
                    dve.bn_stats(stats[:, k, rt, :], src[:, rt, :]).then_inc(ln_stats[k], 1)
                for rt in range(RT):
                    hold(dve, passed, ln_stats[k], at(b, 2, rt + 1))
                    dve.bn_aggr(moments[:, k, rt, :], stats[:, k, rt, :]).then_inc(ln_moments[k], 1)
                dve.wait_ge(ln_rstd[k], at(b, 2, 2))
                for rt in range(RT):
                    dve.tensor_scalar(dst[:, rt, :], src[:, rt, :], moments[:, k, rt, 0:1], rstd[:, k, rt:rt + 1],
                                      ALU.subtract, ALU.mult).then_inc(ln_done[k], 1)

            def ln1(b):
                dve.wait_ge(x_loaded, at(b, 16, 16))
                layernorm(b, 0, x, xn)

            def fourier(b):
                dve.wait_ge(proj_kept, at(b, 26, 12))
                dve.tensor_tensor(prodA, kF, vF, ALU.mult).then_inc(straight, 1)
                dve.wait_ge(lane_fixed, at(b, 6, 3))
                dve.tensor_tensor_scan(KV[:, 0:256], prodA[:, 0:256], prodA[:, 256:512], 0.0, ALU.add, ALU.subtract)\
                   .then_inc(summed, 1)
                dve.tensor_tensor_scan(KV[:, 256:512], prodB[:, 0:256], prodB[:, 256:512], 0.0, ALU.add, ALU.add)\
                   .then_inc(summed, 1)
                dve.wait_ge(summed, at(b, 2, 2))
                dve.wait_ge(proj_kept, at(b, 26, 14))
                dve.tensor_tensor(prodA, KV, qF, ALU.mult).then_inc(straight, 1)
                dve.wait_ge(lane_fixed, at(b, 6, 6))
                dve.tensor_tensor(Q[:, 0:256], prodA[:, 0:256], prodA[:, 256:512], ALU.add).then_inc(Q_ready, 1)
                dve.tensor_tensor(Q[:, 256:512], prodB[:, 256:512], prodB[:, 0:256], ALU.subtract).then_inc(Q_ready, 1)

            def inverse(b):
                dve.wait_ge(inverse_done, at(b, 1, 1))
                dve.tensor_copy(fpower[:, :], TR[:, 0:RT]).then_inc(fpower_kept, 1)
                dve.wait_ge(fnorm_step, at(b, 2, 2))
                dve.reciprocal(fscale[:, :], fnorm[:, :]).then_inc(fscale_ready, 1)
                dve.wait_ge(fscale_ready, at(b, 1, 1))
                for rt in range(RT):
                    dve.scalar_tensor_tensor(x1[:, rt, :], O[:, rt * 256:(rt + 1) * 256], fscale[:, rt:rt + 1],
                                             x[:, rt, :], ALU.mult, ALU.add).then_inc(x1_done, 1)

            def ln2(b):
                dve.wait_ge(x1_done, at(b, 2, 2))
                layernorm(b, 1, x1, xn)

            def head(b, i):
                if i < HEADS:
                    hold(dve, passed, scores_done, at(b, 16, i + 1))
                    if i >= 2:
                        hold(dve, passed, probs_turned, at(b, 16, i - 1))
                    else:
                        dve.wait_ge(ffn_tables, 16 * FFN_LOADS)
                    for rt, (lo, hi) in enumerate(((0, 128), (128, 384))):
                        dve.tensor_tensor_reduce(probs[i % 2][:, lo:hi], S[i % 2][:, lo:hi],
                                                 neg_bias[:, i, (1 - rt) * P:2 * P], 1.0, TOP, ALU.add, ALU.min,
                                                 neg_max[:, i % 2, rt:rt + 1]).then_inc(scores_masked, 1)
                e = i - 1
                if 0 <= e < HEADS and e % 2 == 1:
                    dve.wait_ge(probs_turned, at(b, 16, e + 1))
                    if e >= 2:
                        dve.wait_ge(pv_done, at(b, 16, e - 1))
                    dve.tensor_copy(probsT[e % 2], PT[:, 0:384]).then_inc(probsT_dve, 1)
                e = i - 2
                if 0 <= e < HEADS and e % 2 == 1:
                    m = e // 2
                    dve.wait_ge(pv_done, at(b, 16, e + 1))
                    att = X[m % 2][:, 0:2 * RT * (KEY + 1)].rearrange("p (h t d) -> p h t d", h=2, t=RT)
                    dve.reciprocal(rsum[:, m % 2, :, :], att[:, :, :, KEY]).then_inc(rsum_ready, 1)
                    dve.wait_ge(rsum_ready, at(b, 8, m + 1))
                    if m >= 2:
                        dve.wait_ge(pair_turned, at(b, 8, m - 1))
                    dve.tensor_tensor(pair[m % 2].rearrange("p t (h d) -> p h t d", h=2), att[:, :, :, 0:KEY],
                                      spread(rsum[:, m % 2, :, :], 3, KEY), ALU.mult).then_inc(pair_normed, 1)

            def wo_add(b):
                dve.wait_ge(wo_done, at(b, 1, 1))
                dve.wait_ge(x1_biased, at(b, 1, 1))
                dve.wait_ge(out_ready, at(b, 1, 0))
                dve.tensor_tensor(x2[:, :, :], O[:, :].rearrange("p (t c) -> p t c", t=RT), x1[:, :, :], ALU.add)\
                   .then_inc(x2_done, 1)

            def ln3(c):
                dve.wait_ge(x2_done, at(c, 1, 1))
                dve.wait_ge(result_free, at(c, 1, 1))
                layernorm(c, 2, x2, xn3)
                dve.wait_ge(xn3T_ready, at(c, 1, 1))
                for il in range(4):
                    dst = small[:, :].rearrange("j (s i) -> j s i", i=8)[:, :, 4 + il]
                    dve.tensor_copy(dst, xn3T[il * D1:(il + 1) * D1, 1, :]).then_inc(small_dve, 1)

            def route_top(c, layer):
                step = F1 if layer == 0 else D1
                hold(dve, passed, logits_done, at(c, 2, layer + 1))
                dve.max(top_val[:, :], G[0:F1, 0:EXPERTS]).then_inc(top_found, 1)
                dve.wait_ge(top_found, at(c, 4, 2 * layer + 1))
                dve.tensor_tensor(gap[:, :], top_val[:, 1:2], top_val[:, 0:1], ALU.subtract).then_inc(gap_ready, 1)
                dve.max_index(top_idx[:, :], top_val[:, :], G[0:F1, 0:EXPERTS]).then_inc(top_found, 1)
                dve.wait_ge(top_found, at(c, 4, 2 * layer + 2))
                dve.tensor_scalar(place[:, :], top_idx[:, 0:TOPK], float(step), None, ALU.mult).then_inc(route_step, 1)
                dve.wait_ge(gap_exp, at(c, 2, layer + 1))
                dve.tensor_scalar(den[:, :], egap[:, :], 1.0, None, ALU.add).then_inc(route_step, 1)
                dve.wait_ge(route_step, at(c, 8, 4 * layer + 2))
                dve.reciprocal(prob[:, 0:1], den[:, :]).then_inc(route_step, 1)
                dve.wait_ge(route_step, at(c, 8, 4 * layer + 3))
                dve.tensor_tensor(prob[:, 1:2], egap[:, :], prob[:, 0:1], ALU.mult).then_inc(route_step, 1)
                dve.wait_ge(route_step, at(c, 8, 4 * layer + 4))
                eye = spread(ident[0:F1, 0:TOKENS], 2, TOPK)
                for half, val in enumerate((prob, place)):
                    n = TOKENS * TOPK
                    dve.tensor_tensor(route_diag[:, half * n:(half + 1) * n].rearrange("p (n k) -> p n k", k=TOPK), eye,
                                      spread(val[:, :], 1, TOKENS), ALU.mult).then_inc(route_ready, 1)

            def route_keep(c, layer):
                own = own_up if layer == 0 else own_dn
                w = own.shape[1]
                dve.wait_ge(route_spread, at(c, 2, layer + 1))
                dve.tensor_copy(offsets[:, :], G[0:1, 256:384]).then_inc(offsets_ready, 1)
                dve.tensor_tensor(pm[:, :].rearrange("p (g w) -> p g w", w=w),
                                  G[:, 128:256].rearrange("p (g w) -> p g w", w=w),
                                  spread(own[:, :], 1, TOKENS * TOPK // w), ALU.mult).then_inc(pm_ready, 1)

            def route(c, layer):
                route_top(c, layer)
                route_keep(c, layer)

            def own_rows(c, n, width, per_bank):
                up_layer = n < UP_GROUPS
                g = n if up_layer else n - UP_GROUPS
                dve.wait_ge(first_done, at(c, GROUPS, n + 1))
                if n >= 2:
                    dve.wait_ge(second_done, at(c, GROUPS, n - 1))
                if g == 0:
                    dve.wait_ge(pm_ready, at(c, 2, 1 if up_layer else 2))
                dve.tensor_tensor(W[g % 2][:, :].rearrange("p (s w) -> p s w", w=width),
                                  F[g % 2][:, :].rearrange("p (s w) -> p s w", w=width),
                                  spread(pm[:, g * per_bank:(g + 1) * per_bank], 2, width), ALU.mult).then_inc(W_ready, 1)

            def up(c, g):
                if g < UP_GROUPS:
                    own_rows(c, g, F1, 8)
                if g >= 1:
                    g -= 1
                    dve.wait_ge(second_done, at(c, GROUPS, g + 1))
                    if g >= 2:
                        dve.wait_ge(h_ready, at(c, 32, 2 * g - 2))
                    n = UP_TOK * F1
                    dve.scalar_tensor_tensor(pre[g % 2][:, :].rearrange("p (n o) -> p n o", o=F1),
                                             G[0:F1, 0:n].rearrange("p (n o) -> p n o", o=F1),
                                             scale_up[:, 0:1], spread(bias_up[:, :], 1, UP_TOK),
                                             ALU.mult, ALU.add).then_inc(hidden_in, 1)

            def down(c, g):
                if g < DN_GROUPS:
                    own_rows(c, UP_GROUPS + g, D1, 16)
                if g >= 1:
                    g -= 1
                    dve.wait_ge(second_done, at(c, GROUPS, UP_GROUPS + g + 1))
                    n = DN_TOK * D1
                    dve.scalar_tensor_tensor(small[:, g * n:(g + 1) * n].rearrange("p (n o) -> p n o", o=D1),
                                             G[0:D1, 0:n].rearrange("p (n o) -> p n o", o=D1),
                                             scale_dn[:, 0:1], spread(bias_dn[:, :], 1, DN_TOK),
                                             ALU.mult, ALU.add).then_inc(y_kept, 1)

            def final(c):
                dve.wait_ge(y_kept, at(c, 8, DN_GROUPS))
                parts = small[:, :].rearrange("p (s c i) -> p c s i", c=CT, i=4)
                for il in range(2, 4):
                    dve.tensor_copy(yT[il * D1:(il + 1) * D1, :, :], parts[:, :, :, il]).then_inc(yT_dve, 1)
                dve.wait_ge(y_turned, at(c, 1, 1))
                dve.tensor_tensor(xn3[:, :, :], FA[:, :].rearrange("p (t c) -> p t c", t=RT), x2[:, :, :], ALU.add)\
                   .then_inc(out_ready, 1)

            steps = {"ln1": ln1, "fourier": fourier, "inverse": inverse, "ln2": ln2, "head": head, "wo": wo_add,
                     "ln3": ln3, "route_up": lambda c: route(c, 0), "up": up, "route_dn": lambda c: route(c, 1),
                     "down": down, "final": final}
            both_halves(lambda b, c: go(steps, b, c), dve)


def constants():
    n = np.arange(DIM)
    f = np.arange(P)
    angle = 2.0 * np.pi * np.outer(n, f) / DIM
    half = (-1.0) ** n
    dft = np.concatenate([np.cos(angle), -np.sin(angle)], 1)
    dft[:, P] = half
    inv = np.concatenate([2.0 * np.cos(angle), -2.0 * np.sin(angle)], 1)
    inv[:, 0] = 1.0
    inv[:, P] = half
    inv /= DIM * math.sqrt(DIM)
    weight = np.full((P, 1), 2.0)
    weight[0] = 1.0
    start = 2 ** (-2 ** (-(math.log2(HEADS) - 3)))
    slopes = np.array([start * start ** i for i in range(HEADS)], np.float32)
    rel = ((SEQ - P + np.arange(P))[:, None, None] - np.arange(SEQ)[None, None, :]).astype(np.float32)
    alibi = slopes[None, :, None] * rel
    neg_bias = np.where(rel >= 0, -alibi, np.float32(BIG))
    own_up = np.repeat(np.repeat(np.eye(UP_TOK), D1, 0), TOPK, 1)
    own_dn = np.repeat(np.repeat(np.eye(2), F1, 0), TOPK, 1)
    made = {"dft": dft, "idft": inv.T, "bin_weight": weight, "neg_bias": neg_bias, "own_up": own_up,
            "own_dn": own_dn, "ident": np.eye(P)}
    return {k: np.ascontiguousarray(v, dtype=np.float32) for k, v in made.items()}


def kernel(**inputs):
    import concourse.bacc as bacc
    from concourse.bass_utils import run_bass_kernel_spmd

    a = {k: np.asarray(v) for k, v in inputs.items()}
    E = EXPERTS

    def columns(v):
        return v.reshape(-1, P).T

    arrays = {
        "x": a["x"],
        "ctxT": a["ctx_1024"].transpose(0, 2, 1),
        "Wk": a["L0_attn_Wk"], "Wv": a["L0_attn_Wv"], "Wq": a["L0_attn_Wq"],
        "b_fourier": np.stack([a[f"L0_attn_b{n}"].reshape(2, P).T for n in "kvq"], 2),
        "xWq": a["L0_xattn_Wq"], "xWk": a["L0_xattn_Wk"], "xWv": a["L0_xattn_Wv"], "xWo": a["L0_xattn_Wo"],
        "xbq": columns(a["L0_xattn_bq"]), "xbk": columns(a["L0_xattn_bk"]), "xbv": columns(a["L0_xattn_bv"]),
        "xbo": a["L0_xattn_bo"][None, :],
        "r_up": a["L0_ffn_W_up"].T.reshape(UP_TOK * CT, P, E).transpose(1, 0, 2),
        "r_dn": a["L0_ffn_W_down"].reshape(E, F1 // 2, 2, F1).transpose(2, 3, 1, 0).reshape(P, F1 // 2, E),
        "a_up": np.tile(a["L0_ffn_A_up"].transpose(2, 0, 1).reshape(D1, E * F1), (P // D1, 1)),
        "b_up": a["L0_ffn_B_up"].transpose(2, 0, 1).reshape(D1, E * F1),
        "a_dn": np.tile(a["L0_ffn_A_down"].transpose(2, 0, 1).reshape(F1, E * D1), (P // F1, 1)),
        "b_dn": a["L0_ffn_B_down"].transpose(2, 0, 1).reshape(F1, E * D1),
        "bias_up": a["L0_ffn_bias_up"].reshape(F1, F1).T,
        "bias_dn": a["L0_ffn_bias_down"].reshape(D1, D1).T,
        "scale_up": a["L0_ffn_scale_up"].reshape(1, 1), "scale_dn": a["L0_ffn_scale_down"].reshape(1, 1),
        **constants(),
    }
    arrays = {k: np.ascontiguousarray(v) for k, v in arrays.items()}
    nc = bacc.Bacc("TRN2", target_bir_lowering=False, num_devices=1)
    t = {k: nc.dram_tensor(f"in_{k}", v.shape, mybir.dt.from_np(v.dtype), kind="ExternalInput").ap() for k, v in arrays.items()}
    out = nc.dram_tensor("out", (BATCH, SEQ, DIM), F32, kind="ExternalOutput").ap()
    decoder_layer(nc, t, out)
    r = run_bass_kernel_spmd(nc, [{f"in_{k}": v for k, v in arrays.items()}], core_ids=[0])
    return r.results[0]["out"]
```

```python
import math
from contextlib import ExitStack

import numpy as np

import concourse.bass as bass
from concourse import mybir

F32 = mybir.dt.float32
I32 = mybir.dt.int32
U32 = mybir.dt.uint32
ALU = mybir.AluOpType
ACT = mybir.ActivationFunctionType

P = 128
BATCH, SEQ, DIM = 16, 256, 256
RT = SEQ // P
CT = DIM // P
HEADS, KEY = 16, 64
PAIRS = HEADS // 2
EXPERTS, TOPK = 64, 2
TOKENS = SEQ * DIM // 1024
D1, F1 = 32, 64
UP_TOK = P // D1
UP_GROUPS = TOKENS // UP_TOK
DN_TOK = 8
DN_GROUPS = TOKENS // DN_TOK
UP_SLOTS, DN_SLOTS = 4, 3
GROUPS = UP_GROUPS + DN_GROUPS
CHOOSERS = {"pool": {"up": range(0, 0), "dn": range(0, 5, 2)},
            "dve": {"up": range(0, 2), "dn": range(1, 4, 2)},
            "act": {"up": range(2, 4), "dn": range(5, 8)}}
LOADED = 4
CHOOSE_PARTS = 2
LN_EPS = 1e-5
BIG = 1.0e9
TOP = 3.0e38


def at(b, per_batch, k):
    return b * per_batch + k


def hold(eng, passed, sem, value):
    eng.wait_ge(sem, value)
    eng.sem_inc(passed, 1)


def spread(ap, axis, n):
    wide = ap.unsqueeze(axis)
    shape = list(wide.shape)
    shape[axis] = n
    return wide.to_broadcast(shape)


def decoder_layer(nc, t, out):
    ctx = ExitStack()
    with ctx:
        def sb(name, shape, dt=F32):
            return ctx.enter_context(nc.sbuf_tensor(name, shape, dt))

        def sem(name):
            return ctx.enter_context(nc.semaphore(name))

        ident = sb("ident", [P, P])
        ones = sb("ones", [F1, P])
        wf = sb("wf", [P, CT, 3, 256])
        bf = sb("bf", [P, 2, 4])
        idft = sb("idft", [P, 2, DIM])
        bin_weight = sb("bin_weight", [P, 1])
        wq = sb("wq", [P, CT, HEADS * KEY])
        wk = sb("wk", [P, CT, HEADS * KEY])
        wv = sb("wv", [P, CT, HEADS * KEY])
        wo = sb("wo", [P, PAIRS, DIM])
        bq = sb("bq", [P, PAIRS])
        bq_neg = sb("bq_neg", [P, PAIRS])
        bk = sb("bk", [P, PAIRS])
        bv = sb("bv", [P, PAIRS])
        out_bias = sb("out_bias", [P, DIM])
        neg_bias = sb("neg_bias", [P, HEADS, 2 * P])
        experts = sb("experts", [P, EXPERTS * 2 * F1])
        experts_dn, experts_up = experts[0:F1, 0:EXPERTS * 2 * D1], experts[F1:F1 + D1, :]
        r_up = sb("r_up", [P, 2 * UP_TOK, EXPERTS])
        r_dn = sb("r_dn", [P, F1 // 2, EXPERTS])
        bias_up = sb("bias_up", [P, F1])
        bias_dn = sb("bias_dn", [P, DIM])
        scale_up = sb("scale_up", [P, 1])
        scale_dn = sb("scale_dn", [P, 1])

        x = sb("x", [P, RT, DIM])
        x1 = sb("x1", [P, RT, DIM])
        x2 = sb("x2", [P, RT, DIM])
        ctxT = sb("ctxT", [P, CT, SEQ])
        xn = sb("xn", [P, RT, DIM])
        xnT = sb("xnT", [P, CT, SEQ])
        xn3 = sb("xn3", [P, RT, DIM])
        xn3T = sb("xn3T", [P, CT, SEQ])
        stats = sb("stats", [P, 3, RT, 6])
        moments = sb("moments", [P, 3, RT, 2])
        var_eps = sb("var_eps", [P, 3, RT])
        rstd = sb("rstd", [P, 3, RT])
        root, inv_root = sb("root", [P, RT]), sb("inv_root", [P, RT])
        shared = sb("shared", [P, 6, 512])
        kF, vF, qF, prodA, prodB, KV = (shared[:, i, :] for i in range(6))
        Q, Qsq = kF, vF
        probs = [shared[:, i, 0:384] for i in (0, 1, 5)]
        probsT = [shared[:, i, 0:384] for i in (2, 3)]
        pair = [shared[:, 4, i * 256:(i + 1) * 256].rearrange("p (t d) -> p t d", t=RT) for i in (0, 1)]
        fpower = sb("fpower", [P, RT])
        fnorm = sb("fnorm", [P, RT])
        fscale = sb("fscale", [P, RT])
        qT = sb("qT", [P, PAIRS, SEQ])
        kT = sb("kT", [P, PAIRS, SEQ])
        vals = sb("vals", [P, RT, HEADS, KEY + 1])
        neg_max = sb("neg_max", [P, 3, RT])
        rsum = sb("rsum", [P, 2, 2, RT])
        h = sb("h", [P, TOKENS * F1])
        pre_both = sb("pre", [P, UP_TOK * F1])
        pre = [pre_both[i * F1:(i + 1) * F1, :] for i in (0, 1)]
        own = sb("own", [P, TOKENS * D1])
        A_UP, B_UP = TOPK * UP_TOK * F1, TOPK * F1
        A_DN, B_DN = DN_TOK * TOPK * D1, DN_TOK // 2 * TOPK * D1
        chosen_up = [sb(f"chosen_up{i}", [P, A_UP + B_UP]) for i in range(UP_SLOTS)]
        chosen_dn = [sb(f"chosen_dn{i}", [P, A_DN + B_DN]) for i in range(DN_SLOTS)]
        yT = sb("yT", [P, CT, SEQ])
        W = [sb(f"W{i}", [P, A_DN // 2]) for i in (0, 1)]
        top_val = sb("top_val", [F1, 8])
        top_idx = sb("top_idx", [F1, 8], U32)
        gap = sb("gap", [F1, 1])
        egap = sb("egap", [F1, 1])
        den = sb("den", [F1, 1])
        prob = sb("prob", [F1, TOPK])
        place = sb("place", [F1, TOPK])
        route_diag = sb("route_diag", [F1, 2 * TOKENS * TOPK])
        pm = sb("pm", [P, TOKENS])
        offsets = sb("offsets", [1, TOKENS * TOPK], I32)

        wnat = h[:, 0:1536].rearrange("p (i j c) -> p i j c", i=3, j=2)
        dft = h[:, 1536:2048].rearrange("p (j f) -> p j f", j=2)
        bv_wide = h[:, 2048:3072].rearrange("p (m n) -> p m n", m=PAIRS)
        bnat = h[:, 3072:3078].rearrange("p (j i) -> p j i", j=2)
        bo_row = h[0:1, 3328:3584]

        def bank(name):
            return ctx.enter_context(nc.psum_tensor(name, [P, 512], F32))

        TR, S0, S1, PT, O, FA, FB, G = (bank(n) for n in ("TR", "S0", "S1", "PT", "O", "FA", "FB", "G"))
        S, F, X = [S0, S1], [FA, FB], [O, TR]
        k_banks = v_banks = [S0, S1, PT, O]
        q_banks = [PT, O, FA, FB]

        fourier_tables, attn_tables, ffn_tables = sem("fourier_tables"), sem("attn_tables"), sem("ffn_tables")
        folded, folded_kept, bv_spread, bias_made, vals_ones, exponents = (
            sem("folded"), sem("folded_kept"), sem("bv_spread"), sem("bias_made"), sem("vals_ones"), sem("exponents"))
        x_loaded, ctx_loaded, out_stored = sem("x_loaded"), sem("ctx_loaded"), sem("out_stored")
        ln_stats = [sem(f"ln{i}_stats") for i in (1, 2, 3)]
        ln_moments = [sem(f"ln{i}_moments") for i in (1, 2, 3)]
        ln_rstd = [sem(f"ln{i}_rstd") for i in (1, 2, 3)]
        ln_done = [sem(f"ln{i}_done") for i in (1, 2, 3)]
        xn_turned, xnT_ready = sem("xn_turned"), sem("xnT_ready")
        proj_done = sem("proj_done")
        proj_kept = sem("proj_kept")
        straight, crossed, lane_fixed = sem("straight"), sem("crossed"), sem("lane_fixed")
        summed, Q_ready, Qsq_ready = sem("summed"), sem("Q_ready"), sem("Qsq_ready")
        inverse_done, fpower_kept = sem("inverse_done"), sem("fpower_kept")
        fnorm_step, fscale_ready = sem("fnorm_step"), sem("fscale_ready")
        x1_done, x1_biased, x2_done = sem("x1_done"), sem("x1_biased"), sem("x2_done")
        scores_done, scores_masked, probs_ready = sem("scores_done"), sem("scores_masked"), sem("probs_ready")
        probs_turned, probsT_act, probsT_dve = sem("probs_turned"), sem("probsT_act"), sem("probsT_dve")
        pv_done, rsum_ready, pair_normed = sem("pv_done"), sem("rsum_ready"), sem("pair_normed")
        pair_turned, pair_kept, wo_done = sem("pair_turned"), sem("pair_kept"), sem("wo_done")
        xn3_turned, xn3T_ready = sem("xn3_turned"), sem("xn3T_ready")
        own_act, own_dve = sem("own_act"), sem("own_dve")
        chosen_act, chosen_dve, chosen_pool = sem("chosen_act"), sem("chosen_dve"), sem("chosen_pool")
        zeroed, x2_biased = sem("zeroed"), sem("x2_biased")
        logits_done, top_found, gap_exp = sem("logits_done"), sem("top_found"), sem("gap_exp")
        gap_ready, route_step, route_ready = sem("gap_ready"), sem("route_step"), sem("route_ready")
        route_spread, pm_ready, offsets_ready = sem("route_spread"), sem("pm_ready"), sem("offsets_ready")
        first_done, W_ready, second_done = sem("first_done"), sem("W_ready"), sem("second_done")
        hidden_in, h_ready, y_kept = sem("hidden_in"), sem("h_ready"), sem("y_kept")
        y_turned, out_ready = sem("y_turned"), sem("out_ready")

        result_free = sem("result_free")
        passed = sem("passed")
        FOURIER_LOADS = 6
        ATTN_LOADS = 10
        FFN_LOADS = 9

        block = ctx.enter_context(nc.Block())

        def own_parts(n, il):
            dst = own[n * D1:(n + 1) * D1, :].rearrange("j (g n r c i) -> j n i c g r", n=UP_TOK, r=4, c=CT, i=4)
            src = xn3T[il * D1:(il + 1) * D1, :, :].rearrange("j c (g n r) -> j n c g r", n=UP_TOK, r=4)
            return dst[:, n, il], src[:, n]

        def shares(layer):
            start, found = 0, {}
            for name, share in CHOOSERS.items():
                found[name] = share[layer], start
                start += len(share[layer]) * (UP_GROUPS if layer == "up" else DN_GROUPS) * TOPK
            return found

        def fetch_offsets(held, kind, n, name):
            layer, g, step = ("up", n, 2 * F1) if n < UP_GROUPS else ("dn", n - UP_GROUPS, 2 * D1)
            if g % LOADED:
                return
            tokens, first = shares(layer)[name]
            first += g * len(tokens) * TOPK
            values = nc.values_load_multi_w_load_instructions(
                offsets[0:1, first:first + LOADED * len(tokens) * TOPK], engines=[kind], min_val=0,
                max_val=(EXPERTS - 1) * step,
                skip_runtime_bounds_check_because="an index of one of 64 logits times the table's step")[1]
            for i, value in enumerate(values):
                later, rest = divmod(i, len(tokens) * TOPK)
                held[later, tokens[rest // TOPK], rest % TOPK] = value

        def choose_up(copy, held, g, tokens):
            to = chosen_up[g % UP_SLOTS]
            for n in tokens:
                for k in range(TOPK):
                    a, b = (k * UP_TOK + n) * F1, A_UP + k * F1
                    dst = to[n * D1:(n + 1) * D1, a:a + F1]
                    dst = bass.AP(dst.tensor, dst.offset, [dst.ap[0], [b - a, 2], [1, F1]])
                    src = experts_up[:, bass.ds(held[g % LOADED, n, k], 2 * F1)]
                    last = copy(dst, src.rearrange("p (m c) -> p m c", m=2))
            return last

        def choose_dn(copy, held, g, tokens):
            to = chosen_dn[g % DN_SLOTS]
            for n in tokens:
                u, half = n // 2, n % 2
                for k in range(TOPK):
                    a, b = ((u * TOPK + k) * 2 + half) * D1, A_DN + (u * TOPK + k) * D1
                    dst = to[half * F1:(half + 1) * F1, a:a + D1]
                    dst = bass.AP(dst.tensor, dst.offset, [dst.ap[0], [b - a, 2], [1, D1]])
                    src = experts_dn[:, bass.ds(held[g % LOADED, n, k], 2 * D1)]
                    last = copy(dst, src.rearrange("p (m c) -> p m c", m=2))
            return last

        def both_halves(run, eng):
            run(0, None)
            with eng.Fori(0, BATCH - 1) as c:
                run(c + 1, c)
            run(None, BATCH - 1)

        ORDER = [("ln3_stats", None), ("ln1_stats", None), ("ln3", None), ("k_proj", None), ("ln3_turn", None),
                 ("ln1", None), ("ln1_turn", None), ("logits_up", None), ("route_top_up", None), ("f_proj", None),
                 ("route_up", None), ("choose", (0, 0)), ("v_proj", 0), ("choose", (1, 0)), ("v_proj", 1)]
        beside_up = {0: [("v_proj", 2)], 1: [("v_proj", 3), ("product_kv", None)], 3: [("cumulate", None), ("product_q", None)],
                     5: [("Q", None)], 6: [("inverse", None)], 7: [("power", None)], 8: [("fpower", None)], 10: [("x1", None)],
                     11: [("ln2_stats", None)], 13: [("ln2", None)], 14: [("ln2_turn", None)], 15: [("q_proj", 0)],
                     16: [("q_proj", 1)]}
        for g in range(UP_GROUPS + 1):
            ORDER.append(("up", g))
            if g + 2 < UP_GROUPS:
                ORDER.append(("choose", (g + 2, 0)))
            ORDER += beside_up.get(g, [])
        ORDER += [("logits_dn", None), ("route_top_dn", None)]
        for i in range(HEADS + 5):
            ORDER.append(("head", i))
            if i == 0:
                ORDER += [("q_proj", 2), ("route_dn", None)]
            if i == 1:
                ORDER.append(("q_proj", 3))
            if i < 4:
                ORDER.append(("choose", (UP_GROUPS + i // 2, i % 2)))
            elif (i - 4) // 2 < DN_GROUPS:
                g, second = divmod(i - 4, 2)
                ORDER.append(("dn_second" if second else "dn_first", g))
                if g + 2 < DN_GROUPS:
                    ORDER.append(("choose", (UP_GROUPS + g + 2, second)))
        ORDER += [("wo", None), ("final", None), ("wo_add", None)]
        FFN_STEPS = {"ln3_stats", "ln3", "ln3_turn", "x2_bias", "logits_up", "route_top_up", "route_up", "choose", "up",
                     "logits_dn", "route_top_dn", "route_dn", "dn_first", "dn_second", "final"}

        def go(steps, b, c):
            for name, n in ORDER:
                which = c if name in FFN_STEPS else b
                if which is None or name not in steps:
                    continue
                if n is None:
                    steps[name](which)
                else:
                    steps[name](which, n)

        @block.sync
        def _(sp):
            for dst, src in ((wnat[:, 0], t["Wk"]), (wnat[:, 1], t["Wv"]), (wnat[:, 2], t["Wq"]), (dft, t["dft"])):
                sp.dma_start(dst, src.rearrange("(j p) c -> p j c", p=P)).then_inc(fourier_tables, 16)
            sp.dma_start(bnat, t["b_fourier"]).then_inc(fourier_tables, 16)
            sp.dma_start(ident[:, :], t["ident"]).then_inc(fourier_tables, 16)

            def load(b):
                if not isinstance(b, int) or b > 0:
                    sp.wait_ge(x1_done, at(b, 2, 0))
                    sp.wait_ge(proj_done, at(b, 15, -4))
                sp.dma_start(x[:, :, :], t["x"][b].rearrange("(t p) c -> p t c", p=P)).then_inc(x_loaded, 16)
                sp.dma_start(ctxT[:, :, :], t["ctxT"][b].rearrange("(t p) s -> p t s", p=P)).then_inc(ctx_loaded, 16)

            def store(c):
                sp.wait_ge(out_ready, at(c, 1, 1))
                sp.dma_start(out[c].rearrange("(t p) c -> p t c", p=P), xn3[:, :, :]).then_inc(out_stored, 16)
                sp.wait_ge(out_stored, at(c, 16, 16))
                sp.sem_inc(result_free, 1)

            load(0)
            sp.sem_inc(result_free, 1)
            sp.dma_start(idft[:, :, :], t["idft"].rearrange("(j p) c -> p j c", p=P)).then_inc(attn_tables, 16)
            sp.dma_start(bin_weight[:, :], t["bin_weight"]).then_inc(attn_tables, 16)
            for dst, name in ((wk, "xWk"), (wv, "xWv"), (wq, "xWq"), (wo, "xWo")):
                sp.dma_start(dst[:, :, :], t[name].rearrange("(j p) c -> p j c", p=P)).then_inc(attn_tables, 16)
            for dst, name in ((bq, "xbq"), (bk, "xbk"), (bv, "xbv")):
                sp.dma_start(dst[:, :], t[name]).then_inc(attn_tables, 16)
            sp.dma_start(bo_row, t["xbo"]).then_inc(attn_tables, 16)
            sp.dma_start(neg_bias[:, :, :], t["neg_bias"]).then_inc(ffn_tables, 16)
            for dst, name in ((r_up, "r_up"), (r_dn, "r_dn")):
                sp.dma_start(dst[:, :, :], t[name]).then_inc(ffn_tables, 16)
            for dst, name in ((experts_up, "experts_up"), (experts_dn, "experts_dn"), (bias_up[:, :], "bias_up"),
                              (bias_dn[:, :], "bias_dn")):
                sp.dma_start(dst, t[name]).then_inc(ffn_tables, 16)
            sp.dma_start(scale_up[:, :], t["scale_up"].to_broadcast([P, 1])).then_inc(ffn_tables, 16)
            sp.dma_start(scale_dn[:, :], t["scale_dn"].to_broadcast([P, 1])).then_inc(ffn_tables, 16)

            load(1)
            with sp.Fori(0, BATCH - 2) as c:
                load(c + 2)
                store(c)
            store(BATCH - 2)
            store(BATCH - 1)

        @block.gpsimd
        def _(pool):
            pool.memset(vals[:, :, :, KEY:KEY + 1], 1.0).then_inc(vals_ones, 1)
            pool.memset(ones[:, :], 1.0).then_inc(vals_ones, 1)
            pool.memset(root[:, :], 0.5).then_inc(exponents, 1)
            pool.memset(inv_root[:, :], -0.5).then_inc(exponents, 1)
            for buf in [own] + chosen_up + chosen_dn:
                pool.memset(buf[:, :], 0.0).then_inc(zeroed, 1)
            pool.wait_ge(exponents, 2)
            pool.wait_ge(ffn_tables, 16 * FFN_LOADS)

            def deviation(b, k):
                hold(pool, passed, ln_moments[k], at(b, 2, 2))
                pool.tensor_scalar(var_eps[:, k, :], moments[:, k, :, 1], LN_EPS, None, ALU.add).then_inc(ln_rstd[k], 1)
                pool.wait_ge(ln_rstd[k], at(b, 2, 1))
                pool.tensor_tensor(rstd[:, k, :], var_eps[:, k, :], inv_root[:, :], ALU.pow).then_inc(ln_rstd[k], 1)

            def fpower_root(b):
                pool.wait_ge(fpower_kept, at(b, 1, 1))
                pool.tensor_tensor(fnorm[:, :], fpower[:, :], root[:, :], ALU.pow).then_inc(fnorm_step, 1)
                hold(pool, passed, fnorm_step, at(b, 2, 1))
                pool.tensor_scalar(fnorm[:, :], fnorm[:, :], 1e-9, None, ALU.add).then_inc(fnorm_step, 1)

            def cross(b, k, left, left_sem, left_n, right):
                pool.wait_ge(left_sem, left_n)
                pool.wait_ge(proj_kept, at(b, 26, 12 + 2 * k))
                pool.tensor_tensor(prodB[:, 0:256], left[:, 0:256], right[:, 256:512], ALU.mult).then_inc(crossed, 1)
                pool.tensor_tensor(prodB[:, 256:512], left[:, 256:512], right[:, 0:256], ALU.mult).then_inc(crossed, 1)
                pool.wait_ge(straight, at(b, 2, k + 1))
                hold(pool, passed, crossed, at(b, 4, 2 * k + 2))
                to, zero = (0, 256) if k == 0 else (256, 0)
                pool.tensor_copy(prodB[0:1, to:to + 256], prodA[0:1, 256:512]).then_inc(lane_fixed, 1)
                pool.memset(prodB[0:1, zero:zero + 256], 0.0).then_inc(lane_fixed, 1)
                hold(pool, passed, lane_fixed, at(b, 6, 3 * k + 2))
                pool.memset(prodA[0:1, 256:512], 0.0).then_inc(lane_fixed, 1)

            def bias_x1(b):
                pool.wait_ge(ln_done[1], at(b, 2, 2))
                pool.wait_ge(bias_made, 1)
                pool.tensor_tensor(x1[:, :, :], x1[:, :, :], spread(out_bias[:, :], 1, RT), ALU.add).then_inc(x1_biased, 1)

            def bias_x2(c):
                pool.wait_ge(ln_done[2], at(c, 2, 2))
                pool.tensor_tensor(x2[:, :, :], x2[:, :, :], spread(bias_dn[:, :], 1, RT), ALU.add).then_inc(x2_biased, 1)

            held = {}

            def choose(c, n_part):
                n, part = n_part
                layer = "up" if n < UP_GROUPS else "dn"
                tokens = CHOOSERS["pool"][layer]
                if len(tokens) == 0:
                    return
                if part == 0:
                    fetch_offsets(held, mybir.EngineType.Pool, n, "pool")
                g = n - UP_GROUPS
                if g >= DN_SLOTS and part == 0:
                    hold(pool, passed, second_done, at(c, GROUPS, n - DN_SLOTS + 1))
                cut = (len(tokens) + 1) // CHOOSE_PARTS
                last = choose_dn(pool.tensor_copy, held, g, tokens[:cut] if part == 0 else tokens[cut:])
                if part == CHOOSE_PARTS - 1:
                    last.then_inc(chosen_pool, 1)

            def route(c, layer):
                hold(pool, passed, offsets_ready, at(c, 2, layer + 1))

            steps = {"choose": choose, "route_dn": lambda c: route(c, 1),
                     "ln1": lambda b: deviation(b, 0), "ln2": lambda b: deviation(b, 1), "ln3": lambda c: deviation(c, 2),
                     "product_kv": lambda b: cross(b, 0, kF, proj_kept, at(b, 26, 12), vF),
                     "product_q": lambda b: cross(b, 1, KV, summed, at(b, 2, 2), qF),
                     "fpower": fpower_root, "ln2_turn": bias_x1, "logits_up": bias_x2}
            both_halves(lambda b, c: go(steps, b, c), pool)

        @block.scalar
        def _(act):
            act.wait_ge(folded, 3)
            for i, s in enumerate((S0, S1, PT)):
                act.copy(wf[:, :, i, :], s[:, :].rearrange("p (j f) -> p j f", j=CT)).then_inc(folded_kept, 1)
            act.wait_ge(folded, 4)
            act.copy(bf[:, :, 0:3], TR[:, 0:8].rearrange("p (j i) -> p j i", j=2)[:, :, 0:3]).then_inc(folded_kept, 1)
            act.wait_ge(attn_tables, 16 * ATTN_LOADS)
            act.mul(bq_neg[:, :], bq[:, :], -1.0 / math.sqrt(KEY)).then_inc(folded_kept, 1)
            act.wait_ge(folded, 5)
            act.copy(out_bias[:, :], O[:, 0:DIM]).then_inc(bias_made, 1)
            act.wait_ge(folded_kept, 5)

            def k_proj(b):
                for r in range(4):
                    act.wait_ge(proj_done, at(b, 15, r + 1))
                    for i in range(2):
                        m = 2 * r + i
                        act.activation(kT[:, m, :], k_banks[r][:, i * 256:(i + 1) * 256], ACT.Identity,
                                       bias=bk[:, m:m + 1]).then_inc(proj_kept, 1)

            def keep_xnT(b, k):
                act.wait_ge(xn_turned, at(b, 2, k))
                act.copy(xnT[:, :, :], TR[:, :].rearrange("p (c s) -> p c s", c=CT)).then_inc(xnT_ready, 1)

            def f_proj(b):
                for i, (dst, s) in enumerate(((kF, S0), (vF, S1), (qF, PT))):
                    act.wait_ge(proj_done, at(b, 15, 5 + i))
                    for half in range(2):
                        act.activation(dst[:, half * 256:(half + 1) * 256], s[:, half * 256:(half + 1) * 256],
                                       ACT.Identity, bias=bf[:, half, i:i + 1]).then_inc(proj_kept, 1)

            def v_proj(b, r):
                if isinstance(b, int) and r == 0:
                    act.wait_ge(vals_ones, 2)
                act.wait_ge(proj_done, at(b, 15, 8 + r))
                act.copy(vals[:, r // 2, (r % 2) * 8:(r % 2) * 8 + 8, 0:KEY],
                         v_banks[r][:, :].rearrange("p (h d) -> p h d", d=KEY)).then_inc(proj_kept, 1)

            def inverse(b):
                act.wait_ge(Q_ready, at(b, 2, 2))
                act.activation(Qsq, Q, ACT.Square).then_inc(Qsq_ready, 1)

            def q_proj(b, r):
                act.wait_ge(proj_done, at(b, 15, 12 + r))
                for i in range(2):
                    m = 2 * r + i
                    act.activation(qT[:, m, :], q_banks[r][:, i * 256:(i + 1) * 256], ACT.Identity,
                                   bias=bq_neg[:, m:m + 1], scale=-1.0 / math.sqrt(KEY)).then_inc(proj_kept, 1)

            def head(b, i):
                e = i - 2
                if 0 <= e < HEADS and e % 2 == 0:
                    act.wait_ge(probs_turned, at(b, 16, e + 1))
                    act.copy(probsT[e % 2], PT[:, 0:384]).then_inc(probsT_act, 1)
                if i < HEADS:
                    act.wait_ge(scores_masked, at(b, 32, 2 * i + 2))
                    for rt, (lo, hi) in enumerate(((0, 128), (128, 384))):
                        act.activation(probs[i % 3][:, lo:hi], probs[i % 3][:, lo:hi], ACT.Exp,
                                       bias=neg_max[:, i % 3, rt:rt + 1], scale=-1.0).then_inc(probs_ready, 1)
                if i >= 5 and i % 2 == 1:
                    m = (i - 5) // 2
                    act.wait_ge(pair_turned, at(b, 8, m + 1))
                    act.copy(qT[:, m, :], X[m % 2][:, 0:256]).then_inc(pair_kept, 1)

            def ln3(c):
                act.wait_ge(xn3_turned, at(c, 1, 1))
                act.copy(xn3T[:, :, :], FA[:, :].rearrange("p (c s) -> p c s", c=CT)).then_inc(xn3T_ready, 1)
                act.wait_ge(xn3T_ready, at(c, 1, 1))
                act.wait_ge(zeroed, 1 + UP_SLOTS + DN_SLOTS)
                for n in (0, 1):
                    for il in range(4):
                        act.copy(*own_parts(n, il)).then_inc(own_act, 1)

            def route_exp(c, layer):
                act.wait_ge(gap_ready, at(c, 2, layer + 1))
                act.activation(egap[:, :], gap[:, :], ACT.Exp).then_inc(gap_exp, 1)

            def route(c, layer):
                hold(act, passed, offsets_ready, at(c, 2, layer + 1))

            held = {}

            def choose(c, n_part):
                n, part = n_part
                layer = "up" if n < UP_GROUPS else "dn"
                tokens = CHOOSERS["act"][layer]
                if part == 0:
                    fetch_offsets(held, mybir.EngineType.Activation, n, "act")
                if n < UP_GROUPS:
                    choose_up(act.copy, held, n, tokens).then_inc(chosen_act, 1)
                else:
                    g = n - UP_GROUPS
                    if g >= DN_SLOTS and part == 0:
                        hold(act, passed, second_done, at(c, GROUPS, n - DN_SLOTS + 1))
                    cut = (len(tokens) + 1) // CHOOSE_PARTS
                    last = choose_dn(act.copy, held, g, tokens[:cut] if part == 0 else tokens[cut:])
                    if part == CHOOSE_PARTS - 1:
                        last.then_inc(chosen_act, 1)

            def up(c, g):
                if g == 0:
                    return
                g -= 1
                act.wait_ge(hidden_in, at(c, 16, g + 1))
                cols = slice(g * UP_TOK * F1, (g + 1) * UP_TOK * F1)
                act.activation(h[0:F1, cols], pre[g % 2], ACT.Gelu).then_inc(h_ready, 1)
                above = h[F1:P, cols].rearrange("p (u c) -> p u c", c=2 * F1)[:, :, 0:2 * F1 - F1 // 2]
                shifted = pre[g % 2].rearrange("p (u c) -> p u c", c=2 * F1)[:, :, F1 // 2:2 * F1]
                act.activation(above, shifted, ACT.Gelu).then_inc(h_ready, 1)

            steps = {"k_proj": k_proj, "ln1_turn": lambda b: keep_xnT(b, 1), "f_proj": f_proj, "v_proj": v_proj,
                     "inverse": inverse, "ln2_turn": lambda b: keep_xnT(b, 2), "q_proj": q_proj, "head": head,
                     "ln3_turn": ln3, "route_top_up": lambda c: route_exp(c, 0), "route_up": lambda c: route(c, 0),
                     "up": up, "route_top_dn": lambda c: route_exp(c, 1), "route_dn": lambda c: route(c, 1),
                     "choose": choose}
            both_halves(lambda b, c: go(steps, b, c), act)

        @block.tensor
        def _(pe):
            pe.wait_ge(fourier_tables, 16 * FOURIER_LOADS)
            for i, s in enumerate((S0, S1, PT)):
                for ct in range(CT):
                    for j in range(2):
                        mm = pe.matmul(s[:, ct * 256:(ct + 1) * 256], wnat[:, i, j, ct * P:(ct + 1) * P],
                                       dft[:, j, :], start=(j == 0), stop=(j == 1))
                mm.then_inc(folded, 1)
            for half in range(2):
                for j in range(2):
                    mm = pe.matmul(TR[:, 4 * half:4 * half + 3], dft[:, j, half * P:(half + 1) * P],
                                   bnat[:, j, :], start=(j == 0), stop=(j == 1))
            mm.then_inc(folded, 1)
            pe.wait_ge(attn_tables, 16 * ATTN_LOADS)
            pe.wait_ge(bv_spread, 1)
            pe.wait_ge(vals_ones, 2)
            for m in range(PAIRS):
                pe.matmul(O[:, 0:DIM], bv_wide[:, m, :], wo[:, m, :], start=(m == 0), stop=False)
            pe.matmul(O[:, 0:DIM], ones[0:1, :], bo_row, start=False, stop=True).then_inc(folded, 1)
            pe.wait_ge(folded_kept, 5)
            pe.wait_ge(bias_made, 1)

            def k_proj(b):
                pe.wait_ge(ctx_loaded, at(b, 16, 16))
                pe.wait_ge(scores_masked, at(b, 32, 0))
                pe.wait_ge(probsT_act, at(b, 8, 0))
                pe.wait_ge(probsT_dve, at(b, 8, 0))
                pe.wait_ge(x2_done, at(b, 1, 0))
                for r in range(4):
                    for i in range(2):
                        m = 2 * r + i
                        for ct in range(CT):
                            mm = pe.matmul(k_banks[r][:, i * 256:(i + 1) * 256], wk[:, ct, m * P:(m + 1) * P],
                                           ctxT[:, ct, :], start=(ct == 0), stop=(ct == CT - 1))
                    mm.then_inc(proj_done, 1)

            def turn(b, k):
                pe.wait_ge(ln_done[k - 1], at(b, 2, 2))
                if k == 1:
                    pe.wait_ge(pair_kept, at(b, 8, 0))
                else:
                    pe.wait_ge(x1_done, at(b, 2, 2))
                for ct in range(CT):
                    for rt in range(RT):
                        mm = pe.transpose(TR[:, ct * 256 + rt * P:ct * 256 + (rt + 1) * P],
                                          xn[:, rt, ct * P:(ct + 1) * P], ident[:, :])
                mm.then_inc(xn_turned, 1)

            def f_proj(b):
                pe.wait_ge(xnT_ready, at(b, 2, 1))
                for i, s in enumerate((S0, S1, PT)):
                    pe.wait_ge(proj_kept, at(b, 26, 2 * i + 2))
                    for half in range(2):
                        for ct in range(CT):
                            mm = pe.matmul(s[:, half * 256:(half + 1) * 256], wf[:, ct, i, half * P:(half + 1) * P],
                                           xnT[:, ct, :], start=(ct == 0), stop=(ct == CT - 1))
                    mm.then_inc(proj_done, 1)

            def v_proj(b, r):
                pe.wait_ge(proj_kept, at(b, 26, 10 + 2 * r if r < 3 else 8))
                for ct in range(CT):
                    mm = pe.matmul(v_banks[r][:, :], ctxT[:, ct, (r // 2) * P:(r // 2 + 1) * P],
                                   wv[:, ct, (r % 2) * 512:(r % 2 + 1) * 512], start=(ct == 0), stop=(ct == CT - 1))
                mm.then_inc(proj_done, 1)

            def inverse(b):
                pe.wait_ge(Q_ready, at(b, 2, 2))
                pe.wait_ge(proj_kept, at(b, 26, 18))
                for rt in range(RT):
                    for half in range(2):
                        pe.matmul(O[:, rt * 256:(rt + 1) * 256], Q[:, half * 256 + rt * P:half * 256 + (rt + 1) * P],
                                  idft[:, half, :], start=(half == 0), stop=(half == 1))

            def power(b):
                pe.wait_ge(Qsq_ready, at(b, 1, 1))
                for rt in range(RT):
                    for half in range(2):
                        mm = pe.matmul(TR[:, rt:rt + 1], Qsq[:, half * 256 + rt * P:half * 256 + (rt + 1) * P],
                                       bin_weight[:, :], start=(half == 0), stop=(half == 1))
                mm.then_inc(inverse_done, 1)

            def q_proj(b, r):
                if r == 0:
                    pe.wait_ge(xnT_ready, at(b, 2, 2))
                if r == 1:
                    pe.wait_ge(x1_done, at(b, 2, 2))
                elif r == 0:
                    pe.wait_ge(proj_kept, at(b, 26, 17))
                for i in range(2):
                    m = 2 * r + i
                    for ct in range(CT):
                        mm = pe.matmul(q_banks[r][:, i * 256:(i + 1) * 256], wq[:, ct, m * P:(m + 1) * P],
                                       xnT[:, ct, :], start=(ct == 0), stop=(ct == CT - 1))
                mm.then_inc(proj_done, 1)

            def head(b, i):
                e = i - 3
                if 0 <= e < HEADS:
                    if e % 2 == 0:
                        pe.wait_ge(probsT_act, at(b, 8, e // 2 + 1))
                    else:
                        pe.wait_ge(probsT_dve, at(b, 8, e // 2 + 1))
                e = i - 2
                if 0 <= e < HEADS:
                    pe.wait_ge(probs_ready, at(b, 32, 2 * e + 2))
                    for j in range(3):
                        mm = pe.transpose(PT[:, j * P:(j + 1) * P], probs[e % 3][:, j * P:(j + 1) * P], ident[:, :])
                    mm.then_inc(probs_turned, 1)
                if i < HEADS:
                    m, lo = i // 2, (i % 2) * KEY
                    if i % 4 == 0:
                        pe.wait_ge(proj_kept, at(b, 26, 20 + i // 2))
                    pe.matmul(S[i % 2][:, 0:P], qT[lo:lo + KEY, m, 0:P], kT[lo:lo + KEY, m, 0:P], start=True, stop=True)
                    pe.matmul(S[i % 2][:, P:3 * P], qT[lo:lo + KEY, m, P:2 * P], kT[lo:lo + KEY, m, :],
                              start=True, stop=True).then_inc(scores_done, 1)
                e = i - 3
                if 0 <= e < HEADS:
                    m = e // 2
                    if e % 2 == 0 and m >= 2:
                        pe.wait_ge(pair_kept, at(b, 8, m - 1))
                    to, o = X[m % 2], (e % 2) * RT * (KEY + 1)
                    p = probsT[e % 2]
                    pe.matmul(to[:, o:o + KEY + 1], p[:, 0:P], vals[:, 0, e, :], start=True, stop=True)
                    o += KEY + 1
                    pe.matmul(to[:, o:o + KEY + 1], p[:, P:2 * P], vals[:, 0, e, :], start=True, stop=False)
                    pe.matmul(to[:, o:o + KEY + 1], p[:, 2 * P:3 * P], vals[:, 1, e, :], start=False, stop=True)\
                      .then_inc(pv_done, 1)
                if i >= 5 and i % 2 == 1:
                    turn_pair(b, (i - 5) // 2)

            def turn_pair(b, m):
                pe.wait_ge(pair_normed, at(b, 8, m + 1))
                for rt in range(RT):
                    mm = pe.transpose(X[m % 2][:, rt * P:(rt + 1) * P], pair[m % 2][:, rt, :], ident[:, :])
                mm.then_inc(pair_turned, 1)

            def wo_proj(b):
                pe.wait_ge(pair_kept, at(b, 8, PAIRS - 1))
                for rt in range(RT):
                    for m in range(PAIRS):
                        if rt == 0 and m == PAIRS - 1:
                            pe.wait_ge(pair_kept, at(b, 8, PAIRS))
                        mm = pe.matmul(O[:, rt * 256:(rt + 1) * 256], qT[:, m, rt * P:(rt + 1) * P], wo[:, m, :],
                                       start=(m == 0), stop=(m == PAIRS - 1))
                mm.then_inc(wo_done, 1)

            def ln3(c):
                pe.wait_ge(ln_done[2], at(c, 2, 2))
                for ct in range(CT):
                    for rt in range(RT):
                        mm = pe.transpose(FA[:, ct * 256 + rt * P:ct * 256 + (rt + 1) * P],
                                          xn3[:, rt, ct * P:(ct + 1) * P], ident[:, :])
                mm.then_inc(xn3_turned, 1)

            def logits_up(c):
                pe.wait_ge(xn3T_ready, at(c, 1, 1))
                pe.wait_ge(ffn_tables, 16 * FFN_LOADS)
                for r in range(UP_TOK):
                    for ct in range(CT):
                        n = r * CT + ct
                        rows = xn3T[:, ct, :].rearrange("p (n r) -> p r n", r=UP_TOK)[:, r, :]
                        mm = pe.matmul(G[0:F1, 0:EXPERTS], rows, r_up[:, n, :], start=(n == 0), stop=(n == 2 * UP_TOK - 1))
                mm.then_inc(logits_done, 1)

            def logits_dn(c):
                pe.wait_ge(h_ready, at(c, 32, 32))
                cols = h[:, :].rearrange("p (n two q) -> p two q n", n=TOKENS, two=2)
                for q in range(F1 // 2):
                    mm = pe.matmul(G[0:F1, 0:EXPERTS], cols[:, 0, q, :], r_dn[:, q, :], start=(q == 0), stop=(q == F1 // 2 - 1))
                mm.then_inc(logits_done, 1)

            def route(c, layer):
                pe.wait_ge(route_ready, at(c, 4, 2 * layer + 2))
                pe.matmul(G[:, 128:384], ones[0:F1, :], route_diag[:, :], start=True, stop=True).then_inc(route_spread, 1)

            def up(c, g):
                if g < UP_GROUPS:
                    pe.wait_ge(chosen_act, at(c, GROUPS, g + 1))
                    pe.wait_ge(chosen_dve, at(c, GROUPS, g + 1))
                    if g == 0:
                        pe.wait_ge(own_act, at(c, 8, 8))
                        pe.wait_ge(own_dve, at(c, 8, 8))
                    pe.matmul(F[g % 2][:, 0:B_UP], own[:, g * P:(g + 1) * P], chosen_up[g % UP_SLOTS][:, A_UP:A_UP + B_UP],
                              start=True, stop=True).then_inc(first_done, 1)
                if g >= 1:
                    g -= 1
                    pe.wait_ge(W_ready, at(c, GROUPS, g + 1))
                    if g >= 2:
                        pe.wait_ge(hidden_in, at(c, 16, g - 1))
                    else:
                        pe.wait_ge(pm_ready, at(c, 6, 4))
                    n = UP_TOK * F1
                    for k in range(TOPK):
                        mm = pe.matmul(G[g % 2 * F1:(g % 2 + 1) * F1, 0:n], W[g % 2][:, k * F1:(k + 1) * F1],
                                       chosen_up[g % UP_SLOTS][:, k * n:(k + 1) * n], start=(k == 0), stop=(k == TOPK - 1))
                    mm.then_inc(second_done, 1)

            def dn_first(c, g):
                pe.wait_ge(chosen_act, at(c, GROUPS, UP_GROUPS + g + 1))
                pe.wait_ge(chosen_pool, at(c, DN_GROUPS, g + 1))
                hold(pe, passed, chosen_dve, at(c, GROUPS, UP_GROUPS + g + 1))
                w = TOPK * D1
                for u in range(DN_TOK // 2):
                    both = h[:, (g * DN_TOK // 2 + u) * 2 * F1:(g * DN_TOK // 2 + u + 1) * 2 * F1]
                    for half, token in enumerate((both[0:F1, 0:F1], both[F1:P, F1 // 2:F1 // 2 + F1])):
                        rows = slice(half * F1, (half + 1) * F1)
                        mm = pe.matmul(F[g % 2][rows, u * w:(u + 1) * w], token,
                                       chosen_dn[g % DN_SLOTS][rows, A_DN + u * w:A_DN + (u + 1) * w], start=True, stop=True)
                mm.then_inc(first_done, 1)

            def dn_second(c, g):
                pe.wait_ge(W_ready, at(c, GROUPS, UP_GROUPS + g + 1))
                if g >= 2:
                    pe.wait_ge(y_kept, at(c, 32, 4 * g - 4))
                else:
                    pe.wait_ge(pm_ready, at(c, 6, 6))
                for u in range(DN_TOK // 2):
                    for k in range(TOPK):
                        n = u * TOPK + k
                        mm = pe.matmul(G[g % 2 * F1:g % 2 * F1 + D1, u * 2 * D1:(u + 1) * 2 * D1], W[g % 2][:, n * D1:(n + 1) * D1],
                                       chosen_dn[g % DN_SLOTS][:, n * 2 * D1:(n + 1) * 2 * D1],
                                       start=(k == 0), stop=(k == TOPK - 1))
                mm.then_inc(second_done, 1)

            def final(c):
                pe.wait_ge(y_kept, at(c, 32, 32))
                for rt in range(RT):
                    for ct in range(CT):
                        mm = pe.transpose(FA[:, rt * 256 + ct * P:rt * 256 + (ct + 1) * P],
                                          yT[:, ct, rt * P:(rt + 1) * P], ident[:, :])
                mm.then_inc(y_turned, 1)

            steps = {"k_proj": k_proj, "ln1_turn": lambda b: turn(b, 1), "f_proj": f_proj, "v_proj": v_proj,
                     "inverse": inverse, "power": power, "ln2_turn": lambda b: turn(b, 2), "q_proj": q_proj, "head": head, "wo": wo_proj,
                     "ln3_turn": ln3, "logits_up": logits_up, "route_up": lambda c: route(c, 0), "up": up,
                     "logits_dn": logits_dn, "route_dn": lambda c: route(c, 1), "dn_first": dn_first,
                     "dn_second": dn_second, "final": final}
            both_halves(lambda b, c: go(steps, b, c), pe)

        @block.vector
        def _(dve):
            dve.wait_ge(attn_tables, 16 * ATTN_LOADS)
            dve.tensor_copy(bv_wide, spread(bv[:, :], 2, P)).then_inc(bv_spread, 1)

            def ln_moments_of(b, k, src):
                for rt in range(RT):
                    dve.bn_stats(stats[:, k, rt, :], src[:, rt, :]).then_inc(ln_stats[k], 1)
                for rt in range(RT):
                    hold(dve, passed, ln_stats[k], at(b, 2, rt + 1))
                    dve.bn_aggr(moments[:, k, rt, :], stats[:, k, rt, :]).then_inc(ln_moments[k], 1)

            def layernorm(b, k, src, dst):
                dve.wait_ge(ln_rstd[k], at(b, 2, 2))
                for rt in range(RT):
                    dve.tensor_scalar(dst[:, rt, :], src[:, rt, :], moments[:, k, rt, 0:1], rstd[:, k, rt:rt + 1],
                                      ALU.subtract, ALU.mult).then_inc(ln_done[k], 1)

            def ln1_stats(b):
                dve.wait_ge(x_loaded, at(b, 16, 16))
                ln_moments_of(b, 0, x)

            def product_kv(b):
                dve.wait_ge(proj_kept, at(b, 26, 12))
                dve.tensor_tensor(prodA, kF, vF, ALU.mult).then_inc(straight, 1)

            def cumulate(b):
                dve.wait_ge(lane_fixed, at(b, 6, 3))
                dve.tensor_tensor_scan(KV[:, 0:256], prodA[:, 0:256], prodA[:, 256:512], 0.0, ALU.add, ALU.subtract)\
                   .then_inc(summed, 1)
                dve.tensor_tensor_scan(KV[:, 256:512], prodB[:, 0:256], prodB[:, 256:512], 0.0, ALU.add, ALU.add)\
                   .then_inc(summed, 1)

            def product_q(b):
                dve.wait_ge(summed, at(b, 2, 2))
                dve.wait_ge(proj_kept, at(b, 26, 14))
                dve.tensor_tensor(prodA, KV, qF, ALU.mult).then_inc(straight, 1)

            def spectrum(b):
                dve.wait_ge(lane_fixed, at(b, 6, 6))
                dve.tensor_tensor(Q[:, 0:256], prodA[:, 0:256], prodA[:, 256:512], ALU.add).then_inc(Q_ready, 1)
                dve.tensor_tensor(Q[:, 256:512], prodB[:, 256:512], prodB[:, 0:256], ALU.subtract).then_inc(Q_ready, 1)

            def fpower_keep(b):
                dve.wait_ge(inverse_done, at(b, 1, 1))
                dve.tensor_copy(fpower[:, :], TR[:, 0:RT]).then_inc(fpower_kept, 1)

            def residual1(b):
                dve.wait_ge(fnorm_step, at(b, 2, 2))
                dve.reciprocal(fscale[:, :], fnorm[:, :]).then_inc(fscale_ready, 1)
                dve.wait_ge(fscale_ready, at(b, 1, 1))
                for rt in range(RT):
                    dve.scalar_tensor_tensor(x1[:, rt, :], O[:, rt * 256:(rt + 1) * 256], fscale[:, rt:rt + 1],
                                             x[:, rt, :], ALU.mult, ALU.add).then_inc(x1_done, 1)

            def ln2_stats(b):
                dve.wait_ge(x1_done, at(b, 2, 2))
                ln_moments_of(b, 1, x1)

            def head(b, i):
                e = i - 2
                if 0 <= e < HEADS and e % 2 == 1:
                    dve.wait_ge(probs_turned, at(b, 16, e + 1))
                    dve.tensor_copy(probsT[e % 2], PT[:, 0:384]).then_inc(probsT_dve, 1)
                if i < HEADS:
                    hold(dve, passed, scores_done, at(b, 16, i + 1))
                    if i == 0:
                        dve.wait_ge(ffn_tables, 16 * FFN_LOADS)
                    for rt, (lo, hi) in enumerate(((0, 128), (128, 384))):
                        dve.tensor_tensor_reduce(probs[i % 3][:, lo:hi], S[i % 2][:, lo:hi],
                                                 neg_bias[:, i, (1 - rt) * P:2 * P], 1.0, TOP, ALU.add, ALU.min,
                                                 neg_max[:, i % 3, rt:rt + 1]).then_inc(scores_masked, 1)
                e = i - 3
                if 0 <= e < HEADS and e % 2 == 1:
                    m = e // 2
                    dve.wait_ge(pv_done, at(b, 16, e + 1))
                    att = X[m % 2][:, 0:2 * RT * (KEY + 1)].rearrange("p (h t d) -> p h t d", h=2, t=RT)
                    dve.reciprocal(rsum[:, m % 2, :, :], att[:, :, :, KEY]).then_inc(rsum_ready, 1)
                    dve.wait_ge(rsum_ready, at(b, 8, m + 1))
                    dve.tensor_tensor(pair[m % 2].rearrange("p t (h d) -> p h t d", h=2), att[:, :, :, 0:KEY],
                                      spread(rsum[:, m % 2, :, :], 3, KEY), ALU.mult).then_inc(pair_normed, 1)

            def wo_add(b):
                dve.wait_ge(wo_done, at(b, 1, 1))
                dve.wait_ge(x1_biased, at(b, 1, 1))
                dve.wait_ge(out_ready, at(b, 1, 0))
                dve.tensor_tensor(x2[:, :, :], O[:, :].rearrange("p (t c) -> p t c", t=RT), x1[:, :, :], ALU.add)\
                   .then_inc(x2_done, 1)

            def ln3_stats(c):
                dve.wait_ge(x2_done, at(c, 1, 1))
                ln_moments_of(c, 2, x2)

            def ln3(c):
                dve.wait_ge(result_free, at(c, 1, 1))
                layernorm(c, 2, x2, xn3)

            def spread_tokens(c):
                dve.wait_ge(xn3T_ready, at(c, 1, 1))
                dve.wait_ge(zeroed, 1 + UP_SLOTS + DN_SLOTS)
                for n in (2, 3):
                    for il in range(4):
                        dve.tensor_copy(*own_parts(n, il)).then_inc(own_dve, 1)

            def route_top(c, layer):
                step = 2 * F1 if layer == 0 else 2 * D1
                hold(dve, passed, logits_done, at(c, 2, layer + 1))
                dve.max(top_val[:, :], G[0:F1, 0:EXPERTS]).then_inc(top_found, 1)
                dve.wait_ge(top_found, at(c, 4, 2 * layer + 1))
                dve.tensor_tensor(gap[:, :], top_val[:, 1:2], top_val[:, 0:1], ALU.subtract).then_inc(gap_ready, 1)
                dve.max_index(top_idx[:, :], top_val[:, :], G[0:F1, 0:EXPERTS]).then_inc(top_found, 1)
                dve.wait_ge(top_found, at(c, 4, 2 * layer + 2))
                dve.tensor_scalar(place[:, :], top_idx[:, 0:TOPK], float(step), None, ALU.mult).then_inc(route_step, 1)
                dve.wait_ge(gap_exp, at(c, 2, layer + 1))
                dve.tensor_scalar(den[:, :], egap[:, :], 1.0, None, ALU.add).then_inc(route_step, 1)
                dve.wait_ge(route_step, at(c, 8, 4 * layer + 2))
                dve.reciprocal(prob[:, 0:1], den[:, :]).then_inc(route_step, 1)
                dve.wait_ge(route_step, at(c, 8, 4 * layer + 3))
                dve.tensor_tensor(prob[:, 1:2], egap[:, :], prob[:, 0:1], ALU.mult).then_inc(route_step, 1)
                dve.wait_ge(route_step, at(c, 8, 4 * layer + 4))
                eye = spread(ident[0:F1, 0:TOKENS], 2, TOPK)
                for half, val in enumerate((prob, place)):
                    n = TOKENS * TOPK
                    dve.tensor_tensor(route_diag[:, half * n:(half + 1) * n].rearrange("p (n k) -> p n k", k=TOPK), eye,
                                      spread(val[:, :], 1, TOKENS), ALU.mult).then_inc(route_ready, 1)

            def route_keep(c, layer):
                dve.wait_ge(route_spread, at(c, 2, layer + 1))
                n = UP_TOK if layer == 0 else DN_TOK
                groups = TOKENS // n
                for tokens, start in shares("up" if layer == 0 else "dn").values():
                    if len(tokens) == 0:
                        continue
                    to = offsets[:, start:start + groups * len(tokens) * TOPK]
                    of = G[0:1, 256:384].rearrange("p (g n k) -> p g n k", n=n, k=TOPK)
                    last = dve.tensor_copy(to.rearrange("p (g n k) -> p g n k", g=groups, k=TOPK),
                                           of[:, :, tokens[0]:tokens[-1] + 1:tokens.step, :])
                last.then_inc(offsets_ready, 1)
                n = UP_TOK if layer == 0 else 2
                width, groups = P // n, TOKENS // n
                for j in range(n):
                    rows = slice(j * width, (j + 1) * width)
                    dve.tensor_copy(pm[rows, 0:groups * TOPK].rearrange("p (g k) -> p g k", k=TOPK),
                                    G[rows, 128:256].rearrange("p (g n k) -> p n g k", n=n, k=TOPK)[:, j])\
                       .then_inc(pm_ready, 1)

            def route(c, layer):
                route_keep(c, layer)
                hold(dve, passed, offsets_ready, at(c, 2, layer + 1))

            held = {}

            def choose(c, n_part):
                n, part = n_part
                layer = "up" if n < UP_GROUPS else "dn"
                tokens = CHOOSERS["dve"][layer]
                if part == 0:
                    fetch_offsets(held, mybir.EngineType.DVE, n, "dve")
                if n < UP_GROUPS:
                    choose_up(dve.tensor_copy, held, n, tokens).then_inc(chosen_dve, 1)
                else:
                    g = n - UP_GROUPS
                    cut = (len(tokens) + 1) // CHOOSE_PARTS
                    last = choose_dn(dve.tensor_copy, held, g, tokens[:cut] if part == 0 else tokens[cut:])
                    if part == CHOOSE_PARTS - 1:
                        last.then_inc(chosen_dve, 1)

            def weigh(c, n, width, per_group):
                up_layer = n < UP_GROUPS
                g = n if up_layer else n - UP_GROUPS
                dve.wait_ge(first_done, at(c, GROUPS, n + 1))
                if g == 0:
                    dve.wait_ge(pm_ready, at(c, 6, 4 if up_layer else 6))
                cols = per_group * width
                dve.tensor_tensor(W[g % 2][:, 0:cols].rearrange("p (s w) -> p s w", w=width),
                                  F[g % 2][:, 0:cols].rearrange("p (s w) -> p s w", w=width),
                                  spread(pm[:, g * per_group:(g + 1) * per_group], 2, width), ALU.mult).then_inc(W_ready, 1)

            def up(c, g):
                if g < UP_GROUPS:
                    weigh(c, g, F1, TOPK)
                if g >= 1:
                    g -= 1
                    dve.wait_ge(second_done, at(c, GROUPS, g + 1))
                    if g >= 2:
                        dve.wait_ge(h_ready, at(c, 32, 2 * g - 2))
                    n = UP_TOK * F1
                    side = slice(g % 2 * F1, (g % 2 + 1) * F1)
                    dve.scalar_tensor_tensor(pre[g % 2].rearrange("p (n o) -> p n o", o=F1),
                                             G[side, 0:n].rearrange("p (n o) -> p n o", o=F1),
                                             scale_up[side, 0:1], spread(bias_up[side, :], 1, UP_TOK),
                                             ALU.mult, ALU.add).then_inc(hidden_in, 1)

            def keep_y(c, g):
                dve.wait_ge(second_done, at(c, GROUPS, UP_GROUPS + g + 1))
                rows = DN_TOK * 4
                y = G[g % 2 * F1:g % 2 * F1 + D1, 0:DN_TOK * D1].rearrange("p (s c i) -> p i c s", c=CT, i=4)
                for il in range(4):
                    dve.tensor_copy(yT[il * D1:(il + 1) * D1, :, g * rows:(g + 1) * rows], y[:, il]).then_inc(y_kept, 1)

            def final(c):
                dve.wait_ge(x2_biased, at(c, 1, 1))
                dve.wait_ge(y_turned, at(c, 1, 1))
                dve.scalar_tensor_tensor(xn3[:, :, :], FA[:, :].rearrange("p (t c) -> p t c", t=RT), scale_dn[:, 0:1],
                                         x2[:, :, :], ALU.mult, ALU.add).then_inc(out_ready, 1)

            steps = {"ln1_stats": ln1_stats, "ln1": lambda b: layernorm(b, 0, x, xn), "product_kv": product_kv,
                     "cumulate": cumulate, "product_q": product_q, "Q": spectrum, "fpower": fpower_keep, "x1": residual1,
                     "ln2_stats": ln2_stats, "ln2": lambda b: layernorm(b, 1, x1, xn), "head": head, "wo_add": wo_add,
                     "ln3_stats": ln3_stats, "ln3": ln3, "logits_up": spread_tokens,
                     "route_top_up": lambda c: route_top(c, 0), "route_up": lambda c: route(c, 0), "up": up,
                     "route_top_dn": lambda c: route_top(c, 1), "route_dn": lambda c: route(c, 1),
                     "dn_first": lambda c, g: weigh(c, UP_GROUPS + g, D1, DN_TOK // 2 * TOPK), "dn_second": keep_y,
                     "final": final, "choose": choose}
            both_halves(lambda b, c: go(steps, b, c), dve)


def constants():
    n = np.arange(DIM)
    f = np.arange(P)
    angle = 2.0 * np.pi * np.outer(n, f) / DIM
    half = (-1.0) ** n
    dft = np.concatenate([np.cos(angle), -np.sin(angle)], 1)
    dft[:, P] = half
    inv = np.concatenate([2.0 * np.cos(angle), -2.0 * np.sin(angle)], 1)
    inv[:, 0] = 1.0
    inv[:, P] = half
    inv /= DIM * math.sqrt(DIM)
    weight = np.full((P, 1), 2.0)
    weight[0] = 1.0
    start = 2 ** (-2 ** (-(math.log2(HEADS) - 3)))
    slopes = np.array([start * start ** i for i in range(HEADS)], np.float32)
    rel = ((SEQ - P + np.arange(P))[:, None, None] - np.arange(SEQ)[None, None, :]).astype(np.float32)
    alibi = slopes[None, :, None] * rel
    neg_bias = np.where(rel >= 0, -alibi, np.float32(BIG))
    made = {"dft": dft, "idft": inv.T, "bin_weight": weight, "neg_bias": neg_bias, "ident": np.eye(P)}
    return {k: np.ascontiguousarray(v, dtype=np.float32) for k, v in made.items()}


def kernel(**inputs):
    import concourse.bacc as bacc
    from concourse.bass_utils import run_bass_kernel_spmd

    a = {k: np.asarray(v) for k, v in inputs.items()}
    E = EXPERTS

    def columns(v):
        return v.reshape(-1, P).T

    arrays = {
        "x": a["x"],
        "ctxT": a["ctx_1024"].transpose(0, 2, 1),
        "Wk": a["L0_attn_Wk"], "Wv": a["L0_attn_Wv"], "Wq": a["L0_attn_Wq"],
        "b_fourier": np.stack([a[f"L0_attn_b{n}"].reshape(2, P).T for n in "kvq"], 2),
        "xWq": a["L0_xattn_Wq"], "xWk": a["L0_xattn_Wk"], "xWv": a["L0_xattn_Wv"], "xWo": a["L0_xattn_Wo"],
        "xbq": columns(a["L0_xattn_bq"]), "xbk": columns(a["L0_xattn_bk"]), "xbv": columns(a["L0_xattn_bv"]),
        "xbo": a["L0_xattn_bo"][None, :],
        "r_up": a["L0_ffn_W_up"].T.reshape(UP_TOK * CT, P, E).transpose(1, 0, 2),
        "r_dn": a["L0_ffn_W_down"].reshape(E, 2, F1 // 2, F1).transpose(1, 3, 2, 0).reshape(P, F1 // 2, E),
        "experts_up": np.stack([a["L0_ffn_A_up"], a["L0_ffn_B_up"]], 1).transpose(3, 0, 1, 2).reshape(D1, -1),
        "experts_dn": np.stack([a["L0_ffn_A_down"], a["L0_ffn_B_down"]], 1).transpose(3, 0, 1, 2).reshape(F1, -1),
        "bias_up": np.tile(a["L0_ffn_bias_up"].reshape(F1, F1).T, (2, 1)),
        "bias_dn": np.tile(a["L0_ffn_bias_down"].reshape(4, DIM), (P // 4, 1)),
        "scale_up": a["L0_ffn_scale_up"].reshape(1, 1), "scale_dn": a["L0_ffn_scale_down"].reshape(1, 1),
        **constants(),
    }
    arrays = {k: np.ascontiguousarray(v) for k, v in arrays.items()}
    nc = bacc.Bacc("TRN2", target_bir_lowering=False, num_devices=1)
    t = {k: nc.dram_tensor(f"in_{k}", v.shape, mybir.dt.from_np(v.dtype), kind="ExternalInput").ap() for k, v in arrays.items()}
    out = nc.dram_tensor("out", (BATCH, SEQ, DIM), F32, kind="ExternalOutput").ap()
    decoder_layer(nc, t, out)
    r = run_bass_kernel_spmd(nc, [{f"in_{k}": v for k, v in arrays.items()}], core_ids=[0])
    return r.results[0]["out"]
```

```python
import math
from contextlib import ExitStack

import numpy as np

import concourse.bass as bass
from concourse import mybir

F32 = mybir.dt.float32
I32 = mybir.dt.int32
U32 = mybir.dt.uint32
ALU = mybir.AluOpType
ACT = mybir.ActivationFunctionType

P = 128
BATCH, SEQ, DIM = 16, 256, 256
RT = SEQ // P
CT = DIM // P
HEADS, KEY = 16, 64
PAIRS = HEADS // 2
EXPERTS, TOPK = 64, 2
TOKENS = SEQ * DIM // 1024
D1, F1 = 32, 64
UP_TOK = P // D1
UP_GROUPS = TOKENS // UP_TOK
DN_TOK = 8
DN_GROUPS = TOKENS // DN_TOK
UP_SLOTS, DN_SLOTS = 5, 3
UP_SKEW = 2
GROUPS = UP_GROUPS + DN_GROUPS
CHOOSERS = {"pool": {"up": range(0, 1), "dn": range(0, 0)},
            "dve": {"up": range(1, 4), "dn": range(0, 8)},
            "act": {"up": range(4, 8), "dn": range(8, 16)}}
LOADED = 4
CHOOSE_PARTS = 2
LN_EPS = 1e-5
BIG = 1.0e9
TOP = 3.0e38


def at(b, per_batch, k):
    return b * per_batch + k


def hold(eng, passed, sem, value):
    eng.wait_ge(sem, value)
    eng.sem_inc(passed, 1)


def spread(ap, axis, n):
    wide = ap.unsqueeze(axis)
    shape = list(wide.shape)
    shape[axis] = n
    return wide.to_broadcast(shape)


def decoder_layer(nc, t, out):
    ctx = ExitStack()
    with ctx:
        def sb(name, shape, dt=F32):
            return ctx.enter_context(nc.sbuf_tensor(name, shape, dt))

        def sem(name):
            return ctx.enter_context(nc.semaphore(name))

        ident = sb("ident", [P, P])
        ones = sb("ones", [F1, P])
        wf = sb("wf", [P, CT, 3, 256])
        bf = sb("bf", [P, 2, 4])
        idft = sb("idft", [P, 2, DIM])
        bin_weight = sb("bin_weight", [P, 1])
        wq = sb("wq", [P, CT, HEADS * KEY])
        wk = sb("wk", [P, CT, HEADS * KEY])
        wv = sb("wv", [P, CT, HEADS * KEY])
        wo = sb("wo", [P, PAIRS, DIM])
        bq = sb("bq", [P, PAIRS])
        bq_neg = sb("bq_neg", [P, PAIRS])
        bk = sb("bk", [P, PAIRS])
        bv = sb("bv", [P, PAIRS])
        out_bias = sb("out_bias", [P, DIM])
        neg_bias = sb("neg_bias", [P, HEADS, 2 * P])
        experts = sb("experts", [P, EXPERTS * 2 * F1])
        experts_up, experts_dn = experts[0:D1, :], experts[F1:P, 0:EXPERTS * 2 * D1]
        r_up = sb("r_up", [P, 2 * UP_TOK, EXPERTS])
        r_dn = sb("r_dn", [P, F1 // 2, EXPERTS])
        bias_up = sb("bias_up", [P, F1])
        bias_dn = sb("bias_dn", [P, DIM])
        scale_up = sb("scale_up", [P, 1])
        scale_dn = sb("scale_dn", [P, 1])

        x = sb("x", [P, RT, DIM])
        x1 = sb("x1", [P, RT, DIM])
        x2 = sb("x2", [P, RT, DIM])
        ctxT = sb("ctxT", [P, CT, SEQ])
        xn = sb("xn", [P, RT, DIM])
        xnT = sb("xnT", [P, CT, SEQ])
        xn3 = sb("xn3", [P, RT, DIM])
        xn3T = sb("xn3T", [P, CT, SEQ])
        stats = sb("stats", [P, 3, RT, 6])
        moments = sb("moments", [P, 3, RT, 2])
        var_eps = sb("var_eps", [P, 3, RT])
        rstd = sb("rstd", [P, 3, RT])
        root, inv_root = sb("root", [P, RT]), sb("inv_root", [P, RT])
        shared = sb("shared", [P, 6, 512])
        kF, vF, qF, prodA, prodB, KV = (shared[:, i, :] for i in range(6))
        Q, Qsq = kF, vF
        probs = [shared[:, i, 0:384] for i in (0, 1, 5)]
        probsT = [shared[:, i, 0:384] for i in (2, 3)]
        pair = [shared[:, 4, i * 256:(i + 1) * 256].rearrange("p (t d) -> p t d", t=RT) for i in (0, 1)]
        fpower = sb("fpower", [P, RT])
        fnorm = sb("fnorm", [P, RT])
        fscale = sb("fscale", [P, RT])
        qT = sb("qT", [P, PAIRS, SEQ])
        kT = sb("kT", [P, PAIRS, SEQ])
        vals = sb("vals", [P, RT, HEADS, KEY + 1])
        neg_max = sb("neg_max", [P, 3, RT])
        rsum = sb("rsum", [P, 2, 2, RT])
        h = sb("h", [P, TOKENS * F1])
        pre_both = sb("pre", [P, UP_TOK * F1])
        pre = [pre_both[i * F1:(i + 1) * F1, :] for i in (0, 1)]
        own = sb("own", [P, TOKENS * D1])
        A_UP, B_UP = TOPK * UP_TOK * F1, TOPK * F1
        A_DN, B_DN = DN_TOK * TOPK * D1, DN_TOK // 2 * TOPK * D1
        chosen_up = [sb(f"chosen_up{i}", [P, A_UP + B_UP]) for i in range(UP_SLOTS)]
        chosen_dn = [sb(f"chosen_dn{i}", [P, A_DN + B_DN]) for i in range(DN_SLOTS)]
        yT = sb("yT", [P, CT, SEQ])
        W = [sb(f"W{i}", [P, A_DN // 2]) for i in (0, 1)]
        top_val = sb("top_val", [F1, 8])
        top_idx = sb("top_idx", [F1, 8], U32)
        gap = sb("gap", [F1, 1])
        egap = sb("egap", [F1, 1])
        den = sb("den", [F1, 1])
        prob = sb("prob", [F1, TOPK])
        place = sb("place", [F1, TOPK])
        route_diag = sb("route_diag", [F1, 2 * TOKENS * TOPK])
        pm = sb("pm", [P, TOKENS])
        offsets = sb("offsets", [1, TOKENS * TOPK], I32)

        wnat = h[:, 0:1536].rearrange("p (i j c) -> p i j c", i=3, j=2)
        dft = h[:, 1536:2048].rearrange("p (j f) -> p j f", j=2)
        bv_wide = h[:, 2048:3072].rearrange("p (m n) -> p m n", m=PAIRS)
        bnat = h[:, 3072:3078].rearrange("p (j i) -> p j i", j=2)
        bo_row = h[0:1, 3328:3584]

        def bank(name):
            return ctx.enter_context(nc.psum_tensor(name, [P, 512], F32))

        TR, S0, S1, PT, O, FA, FB, G = (bank(n) for n in ("TR", "S0", "S1", "PT", "O", "FA", "FB", "G"))
        S, F, X = [S0, S1], [FA, FB], [O, TR]
        up_F = [FA, FB, S0]
        k_banks = v_banks = [S0, S1, PT, O]
        q_banks = [PT, O, FA, FB]

        fourier_tables, key_tables, attn_tables, ffn_tables = (
            sem("fourier_tables"), sem("key_tables"), sem("attn_tables"), sem("ffn_tables"))
        folded, folded_kept, bv_spread, bias_made, vals_ones, exponents = (
            sem("folded"), sem("folded_kept"), sem("bv_spread"), sem("bias_made"), sem("vals_ones"), sem("exponents"))
        x_loaded, ctx_loaded, out_stored = sem("x_loaded"), sem("ctx_loaded"), sem("out_stored")
        ln_stats = [sem(f"ln{i}_stats") for i in (1, 2, 3)]
        ln_moments = [sem(f"ln{i}_moments") for i in (1, 2, 3)]
        ln_rstd = [sem(f"ln{i}_rstd") for i in (1, 2, 3)]
        ln_done = [sem(f"ln{i}_done") for i in (1, 2, 3)]
        xn_turned, xnT_ready = sem("xn_turned"), sem("xnT_ready")
        proj_done = sem("proj_done")
        proj_kept = sem("proj_kept")
        straight, crossed, lane_fixed = sem("straight"), sem("crossed"), sem("lane_fixed")
        summed, Q_ready, Qsq_ready = sem("summed"), sem("Q_ready"), sem("Qsq_ready")
        inverse_done, fpower_kept = sem("inverse_done"), sem("fpower_kept")
        fnorm_step, fscale_ready = sem("fnorm_step"), sem("fscale_ready")
        x1_done, x1_biased, x2_done = sem("x1_done"), sem("x1_biased"), sem("x2_done")
        scores_done, scores_masked, probs_ready = sem("scores_done"), sem("scores_masked"), sem("probs_ready")
        probs_turned, probsT_act, probsT_dve = sem("probs_turned"), sem("probsT_act"), sem("probsT_dve")
        pv_done, rsum_ready, pair_normed = sem("pv_done"), sem("rsum_ready"), sem("pair_normed")
        pair_turned, pair_kept, wo_done = sem("pair_turned"), sem("pair_kept"), sem("wo_done")
        xn3_turned, xn3T_ready = sem("xn3_turned"), sem("xn3T_ready")
        own_act, own_dve = sem("own_act"), sem("own_dve")
        chosen_act, chosen_dve, chosen_pool = sem("chosen_act"), sem("chosen_dve"), sem("chosen_pool")
        zeroed, x2_biased = sem("zeroed"), sem("x2_biased")
        logits_done, top_found, gap_exp = sem("logits_done"), sem("top_found"), sem("gap_exp")
        gap_ready, route_step, route_ready = sem("gap_ready"), sem("route_step"), sem("route_ready")
        route_spread, pm_ready, offsets_ready = sem("route_spread"), sem("pm_ready"), sem("offsets_ready")
        first_done, W_ready, second_done = sem("first_done"), sem("W_ready"), sem("second_done")
        hidden_in, h_ready, y_kept = sem("hidden_in"), sem("h_ready"), sem("y_kept")
        y_turned, out_ready = sem("y_turned"), sem("out_ready")

        result_free = sem("result_free")
        passed = sem("passed")
        FOURIER_LOADS = 6
        KEY_LOADS = 6
        ATTN_LOADS = 4
        FFN_LOADS = 9

        block = ctx.enter_context(nc.Block())

        def own_parts(n, il):
            dst = own[n * D1:(n + 1) * D1, :].rearrange("j (g n r c i) -> j n i c g r", n=UP_TOK, r=4, c=CT, i=4)
            src = xn3T[il * D1:(il + 1) * D1, :, :].rearrange("j c (g n r) -> j n c g r", n=UP_TOK, r=4)
            return dst[:, n, il], src[:, n]

        def up_W(g):
            start = g // 2 % 2 * B_UP
            return W[g % 2][:, start:start + B_UP]

        def share_of(name, layer):
            units = CHOOSERS[name][layer]
            return units, units.start * (UP_GROUPS if layer == "up" else DN_GROUPS)

        def fetch_offsets(held, kind, n, name):
            layer, g, step = ("up", n, 2 * F1) if n < UP_GROUPS else ("dn", n - UP_GROUPS, 2 * D1)
            if g % LOADED:
                return
            units, first = share_of(name, layer)
            first += g * len(units)
            values = nc.values_load_multi_w_load_instructions(
                offsets[0:1, first:first + LOADED * len(units)], engines=[kind], min_val=0, max_val=(EXPERTS - 1) * step,
                skip_runtime_bounds_check_because="an index of one of 64 logits times the table's step")[1]
            for i, value in enumerate(values):
                later, unit = divmod(i, len(units))
                held[later, units[unit]] = value

        def choose_up(copy, held, g, units):
            to = chosen_up[g % UP_SLOTS]
            for unit in units:
                n, k = divmod(unit, TOPK)
                a, b = (k * UP_TOK + n) * F1, A_UP + k * F1
                dst = to[n * D1:(n + 1) * D1, a:a + F1]
                dst = bass.AP(dst.tensor, dst.offset, [dst.ap[0], [b - a, 2], [1, F1]])
                src = experts_up[:, bass.ds(held[g % LOADED, unit], 2 * F1)]
                last = copy(dst, src.rearrange("p (m c) -> p m c", m=2))
            return last

        def choose_dn(copy, held, g, units):
            to = chosen_dn[g % DN_SLOTS]
            for unit in units:
                n, k = divmod(unit, TOPK)
                u, half = n // 2, n % 2
                a, b = ((u * TOPK + k) * 2 + half) * D1, A_DN + (u * TOPK + k) * D1
                dst = to[half * F1:(half + 1) * F1, a:a + D1]
                dst = bass.AP(dst.tensor, dst.offset, [dst.ap[0], [b - a, 2], [1, D1]])
                src = experts_dn[:, bass.ds(held[g % LOADED, unit], 2 * D1)]
                last = copy(dst, src.rearrange("p (m c) -> p m c", m=2))
            return last

        def both_halves(run, eng):
            run(0, None)
            with eng.Fori(0, BATCH - 1) as c:
                run(c + 1, c)
            run(None, BATCH - 1)

        ORDER = [("ln3_stats", None), ("ln1_stats", None), ("ln3", None), ("ln1", None),
                 ("k_proj", 0), ("k_proj", 1), ("k_proj", 2), ("ln3_turn", None), ("ln1_turn", None), ("k_proj", 3),
                 ("logits_up", None), ("route_top_up", None), ("f_proj", 0), ("f_proj", 1), ("product_kv", None), ("route_up", None),
                 ("choose", (0, 0)), ("f_proj", 2), ("choose", (1, 0)), ("cumulate", None), ("v_proj", 0),
                 ("product_q", None), ("v_proj", 1), ("choose", (2, 0))]
        beside_up = {0: [("v_proj", 2)], 1: [("v_proj", 3), ("Q", None)], 3: [("inverse", None)], 6: [("power", None)],
                     7: [("fpower", None)], 9: [("x1", 0), ("x1", 1)], 10: [("ln2_stats", 0), ("ln2_stats", 1)],
                     12: [("ln2", 0), ("ln2", 1)], 14: [("ln2_turn", None)], 16: [("q_proj", 0)], 17: [("q_proj", 1)]}
        for g in range(UP_GROUPS + UP_SKEW):
            ORDER.append(("up", g))
            if g + 3 < UP_GROUPS:
                ORDER.append(("choose", (g + 3, 0)))
            ORDER += beside_up.get(g, [])
        ORDER += [("logits_dn", None), ("route_top_dn", None)]
        for i in range(HEADS + 4):
            ORDER.append(("head", i))
            if i == 0:
                ORDER += [("q_proj", 2), ("route_dn", None)]
            if i == 1:
                ORDER.append(("q_proj", 3))
            if 2 <= i < 2 + 2 * DN_GROUPS:
                ORDER.append(("choose", (UP_GROUPS + (i - 2) // 2, i % 2)))
            if i >= 5:
                ORDER.append(("dn_second" if i % 2 == 0 else "dn_first", (i - 5) // 2))
        ORDER += [("wo", 0), ("dn_second", DN_GROUPS - 1), ("wo", 1), ("final", None), ("wo_add", None)]
        FFN_STEPS = {"ln3_stats", "ln3", "ln3_turn", "x2_bias", "logits_up", "route_top_up", "route_up", "choose", "up",
                     "logits_dn", "route_top_dn", "route_dn", "dn_first", "dn_second", "final"}

        def go(steps, b, c):
            for name, n in ORDER:
                which = c if name in FFN_STEPS else b
                if which is None or name not in steps:
                    continue
                if n is None:
                    steps[name](which)
                else:
                    steps[name](which, n)

        @block.sync
        def _(sp):
            for dst, src in ((wnat[:, 0], t["Wk"]), (wnat[:, 1], t["Wv"]), (wnat[:, 2], t["Wq"]), (dft, t["dft"])):
                sp.dma_start(dst, src.rearrange("(j p) c -> p j c", p=P)).then_inc(fourier_tables, 16)
            sp.dma_start(bnat, t["b_fourier"]).then_inc(fourier_tables, 16)
            sp.dma_start(ident[:, :], t["ident"]).then_inc(fourier_tables, 16)

            def load(b):
                if not isinstance(b, int) or b > 0:
                    sp.wait_ge(x1_done, at(b, 2, 0))
                    sp.wait_ge(proj_done, at(b, 15, -4))
                sp.dma_start(x[:, :, :], t["x"][b].rearrange("(t p) c -> p t c", p=P)).then_inc(x_loaded, 16)
                sp.dma_start(ctxT[:, :, :], t["ctxT"][b].rearrange("(t p) s -> p t s", p=P)).then_inc(ctx_loaded, 16)

            def store(c):
                sp.wait_ge(out_ready, at(c, 1, 1))
                sp.dma_start(out[c].rearrange("(t p) c -> p t c", p=P), xn3[:, :, :]).then_inc(out_stored, 16)
                sp.wait_ge(out_stored, at(c, 16, 16))
                sp.sem_inc(result_free, 1)

            load(0)
            sp.sem_inc(result_free, 1)
            for dst, name in ((wk, "xWk"), (wo, "xWo")):
                sp.dma_start(dst[:, :, :], t[name].rearrange("(j p) c -> p j c", p=P)).then_inc(key_tables, 16)
            for dst, name in ((bq, "xbq"), (bk, "xbk"), (bv, "xbv")):
                sp.dma_start(dst[:, :], t[name]).then_inc(key_tables, 16)
            sp.dma_start(bo_row, t["xbo"]).then_inc(key_tables, 16)
            sp.dma_start(idft[:, :, :], t["idft"].rearrange("(j p) c -> p j c", p=P)).then_inc(attn_tables, 16)
            sp.dma_start(bin_weight[:, :], t["bin_weight"]).then_inc(attn_tables, 16)
            for dst, name in ((wv, "xWv"), (wq, "xWq")):
                sp.dma_start(dst[:, :, :], t[name].rearrange("(j p) c -> p j c", p=P)).then_inc(attn_tables, 16)
            sp.dma_start(neg_bias[:, :, :], t["neg_bias"]).then_inc(ffn_tables, 16)
            for dst, name in ((r_up, "r_up"), (r_dn, "r_dn")):
                sp.dma_start(dst[:, :, :], t[name]).then_inc(ffn_tables, 16)
            for dst, name in ((experts_up, "experts_up"), (experts_dn, "experts_dn"), (bias_up[:, :], "bias_up"),
                              (bias_dn[:, :], "bias_dn")):
                sp.dma_start(dst, t[name]).then_inc(ffn_tables, 16)
            sp.dma_start(scale_up[:, :], t["scale_up"].to_broadcast([P, 1])).then_inc(ffn_tables, 16)
            sp.dma_start(scale_dn[:, :], t["scale_dn"].to_broadcast([P, 1])).then_inc(ffn_tables, 16)

            load(1)
            with sp.Fori(0, BATCH - 2) as c:
                load(c + 2)
                store(c)
            store(BATCH - 2)
            store(BATCH - 1)

        @block.gpsimd
        def _(pool):
            pool.memset(vals[:, :, :, KEY:KEY + 1], 1.0).then_inc(vals_ones, 1)
            pool.memset(ones[:, :], 1.0).then_inc(vals_ones, 1)
            pool.memset(root[:, :], 0.5).then_inc(exponents, 1)
            pool.memset(inv_root[:, :], -0.5).then_inc(exponents, 1)
            for buf in [own] + chosen_up + chosen_dn:
                pool.memset(buf[:, :], 0.0).then_inc(zeroed, 1)
            pool.wait_ge(exponents, 2)

            def deviation(b, k):
                hold(pool, passed, ln_moments[k], at(b, 2, 2))
                pool.tensor_scalar(var_eps[:, k, :], moments[:, k, :, 1], LN_EPS, None, ALU.add).then_inc(ln_rstd[k], 1)
                pool.wait_ge(ln_rstd[k], at(b, 2, 1))
                pool.tensor_tensor(rstd[:, k, :], var_eps[:, k, :], inv_root[:, :], ALU.pow).then_inc(ln_rstd[k], 1)

            def fpower_root(b):
                pool.wait_ge(fpower_kept, at(b, 1, 1))
                pool.tensor_tensor(fnorm[:, :], fpower[:, :], root[:, :], ALU.pow).then_inc(fnorm_step, 1)
                hold(pool, passed, fnorm_step, at(b, 2, 1))
                pool.tensor_scalar(fnorm[:, :], fnorm[:, :], 1e-9, None, ALU.add).then_inc(fnorm_step, 1)

            def cross(b, k, left, left_sem, left_n, right):
                pool.wait_ge(left_sem, left_n)
                pool.wait_ge(proj_kept, at(b, 26, 12 + 2 * k))
                pool.tensor_tensor(prodB[:, 0:256], left[:, 0:256], right[:, 256:512], ALU.mult).then_inc(crossed, 1)
                pool.tensor_tensor(prodB[:, 256:512], left[:, 256:512], right[:, 0:256], ALU.mult).then_inc(crossed, 1)
                pool.wait_ge(straight, at(b, 2, k + 1))
                hold(pool, passed, crossed, at(b, 4, 2 * k + 2))
                to, zero = (0, 256) if k == 0 else (256, 0)
                pool.tensor_copy(prodB[0:1, to:to + 256], prodA[0:1, 256:512]).then_inc(lane_fixed, 1)
                pool.memset(prodB[0:1, zero:zero + 256], 0.0).then_inc(lane_fixed, 1)
                hold(pool, passed, lane_fixed, at(b, 6, 3 * k + 2))
                pool.memset(prodA[0:1, 256:512], 0.0).then_inc(lane_fixed, 1)

            def bias_x1(b):
                pool.wait_ge(ln_done[1], at(b, 2, 2))
                pool.wait_ge(bias_made, 1)
                pool.tensor_tensor(x1[:, :, :], x1[:, :, :], spread(out_bias[:, :], 1, RT), ALU.add).then_inc(x1_biased, 1)

            def bias_x2(c):
                pool.wait_ge(ffn_tables, 16 * FFN_LOADS)
                pool.wait_ge(ln_done[2], at(c, 2, 2))
                pool.tensor_tensor(x2[:, :, :], x2[:, :, :], spread(bias_dn[:, :], 1, RT), ALU.add).then_inc(x2_biased, 1)

            held = {}

            def choose(c, n_part):
                n = n_part[0]
                if n < UP_GROUPS:
                    fetch_offsets(held, mybir.EngineType.Pool, n, "pool")
                    if n >= UP_SLOTS:
                        hold(pool, passed, second_done, at(c, GROUPS, n - UP_SLOTS + 1))
                    choose_up(pool.tensor_copy, held, n, CHOOSERS["pool"]["up"]).then_inc(chosen_pool, 1)

            def route_up(c):
                hold(pool, passed, offsets_ready, at(c, 2, 1))

            steps = {"choose": choose, "route_up": route_up,
                     "ln1": lambda b: deviation(b, 0), "ln3": lambda c: deviation(c, 2),
                     "ln2": lambda b, rt: deviation(b, 1) if rt == 0 else None,
                     "product_kv": lambda b: cross(b, 0, kF, proj_kept, at(b, 26, 12), vF),
                     "product_q": lambda b: cross(b, 1, KV, summed, at(b, 2, 2), qF),
                     "fpower": fpower_root, "ln2_turn": bias_x1, "logits_up": bias_x2}
            both_halves(lambda b, c: go(steps, b, c), pool)

        @block.scalar
        def _(act):
            act.wait_ge(folded, 3)
            for i, s in enumerate((S0, S1, PT)):
                act.copy(wf[:, :, i, :], s[:, :].rearrange("p (j f) -> p j f", j=CT)).then_inc(folded_kept, 1)
            act.wait_ge(folded, 4)
            act.copy(bf[:, :, 0:3], TR[:, 0:8].rearrange("p (j i) -> p j i", j=2)[:, :, 0:3]).then_inc(folded_kept, 1)
            act.wait_ge(key_tables, 16 * KEY_LOADS)
            act.mul(bq_neg[:, :], bq[:, :], -1.0 / math.sqrt(KEY)).then_inc(folded_kept, 1)
            act.wait_ge(folded, 5)
            act.copy(out_bias[:, :], O[:, 0:DIM]).then_inc(bias_made, 1)
            act.wait_ge(folded_kept, 5)

            def k_proj(b, r):
                act.wait_ge(proj_done, at(b, 15, r + 1))
                for i in range(2):
                    m = 2 * r + i
                    act.activation(kT[:, m, :], k_banks[r][:, i * 256:(i + 1) * 256], ACT.Identity,
                                   bias=bk[:, m:m + 1]).then_inc(proj_kept, 1)

            def keep_xnT(b, k):
                act.wait_ge(xn_turned, at(b, 2, k))
                act.copy(xnT[:, :, :], TR[:, :].rearrange("p (c s) -> p c s", c=CT)).then_inc(xnT_ready, 1)

            def f_proj(b, i):
                dst, s = (kF, vF, qF)[i], (S0, S1, PT)[i]
                act.wait_ge(proj_done, at(b, 15, 5 + i))
                for half in range(2):
                    act.activation(dst[:, half * 256:(half + 1) * 256], s[:, half * 256:(half + 1) * 256],
                                   ACT.Identity, bias=bf[:, half, i:i + 1]).then_inc(proj_kept, 1)

            def v_proj(b, r):
                if isinstance(b, int) and r == 0:
                    act.wait_ge(vals_ones, 2)
                act.wait_ge(proj_done, at(b, 15, 8 + r))
                act.copy(vals[:, r // 2, (r % 2) * 8:(r % 2) * 8 + 8, 0:KEY],
                         v_banks[r][:, :].rearrange("p (h d) -> p h d", d=KEY)).then_inc(proj_kept, 1)

            def inverse(b):
                act.wait_ge(Q_ready, at(b, 2, 2))
                act.activation(Qsq, Q, ACT.Square).then_inc(Qsq_ready, 1)

            def q_proj(b, r):
                act.wait_ge(proj_done, at(b, 15, 12 + r))
                for i in range(2):
                    m = 2 * r + i
                    act.activation(qT[:, m, :], q_banks[r][:, i * 256:(i + 1) * 256], ACT.Identity,
                                   bias=bq_neg[:, m:m + 1], scale=-1.0 / math.sqrt(KEY)).then_inc(proj_kept, 1)

            def head(b, i):
                e = i - 2
                if 0 <= e < HEADS and e % 2 == 0:
                    act.wait_ge(probs_turned, at(b, 16, e + 1))
                    act.copy(probsT[e % 2], PT[:, 0:384]).then_inc(probsT_act, 1)
                if i < HEADS:
                    act.wait_ge(scores_masked, at(b, 32, 2 * i + 2))
                    for rt, (lo, hi) in enumerate(((0, 128), (128, 384))):
                        act.activation(probs[i % 3][:, lo:hi], probs[i % 3][:, lo:hi], ACT.Exp,
                                       bias=neg_max[:, i % 3, rt:rt + 1], scale=-1.0).then_inc(probs_ready, 1)
                if i >= 5 and i % 2 == 1:
                    m = (i - 5) // 2
                    act.wait_ge(pair_turned, at(b, 8, m + 1))
                    act.copy(qT[:, m, :], X[m % 2][:, 0:256]).then_inc(pair_kept, 1)

            def ln3(c):
                act.wait_ge(xn3_turned, at(c, 1, 1))
                act.copy(xn3T[:, :, :], FA[:, :].rearrange("p (c s) -> p c s", c=CT)).then_inc(xn3T_ready, 1)

            def spread_tokens(c):
                act.wait_ge(xn3T_ready, at(c, 1, 1))
                act.wait_ge(zeroed, 1 + UP_SLOTS + DN_SLOTS)
                for n in (0, 1):
                    for il in range(4):
                        act.copy(*own_parts(n, il)).then_inc(own_act, 1)

            def route_exp(c, layer):
                act.wait_ge(gap_ready, at(c, 2, layer + 1))
                act.activation(egap[:, :], gap[:, :], ACT.Exp).then_inc(gap_exp, 1)

            def route(c, layer):
                hold(act, passed, offsets_ready, at(c, 2, layer + 1))

            held = {}

            def choose(c, n_part):
                n, part = n_part
                layer = "up" if n < UP_GROUPS else "dn"
                units = CHOOSERS["act"][layer]
                if part == 0:
                    fetch_offsets(held, mybir.EngineType.Activation, n, "act")
                if n < UP_GROUPS:
                    choose_up(act.copy, held, n, units).then_inc(chosen_act, 1)
                else:
                    g = n - UP_GROUPS
                    if g >= DN_SLOTS and part == 0:
                        hold(act, passed, second_done, at(c, GROUPS, n - DN_SLOTS + 1))
                    cut = len(units) // CHOOSE_PARTS
                    last = choose_dn(act.copy, held, g, units[:cut] if part == 0 else units[cut:])
                    if part == CHOOSE_PARTS - 1:
                        last.then_inc(chosen_act, 1)

            def up(c, g):
                g -= UP_SKEW
                if g < 0:
                    return
                act.wait_ge(hidden_in, at(c, 16, g + 1))
                cols = slice(g * UP_TOK * F1, (g + 1) * UP_TOK * F1)
                act.activation(h[0:F1, cols], pre[g % 2], ACT.Gelu).then_inc(h_ready, 1)
                above = h[F1:P, cols].rearrange("p (u c) -> p u c", c=2 * F1)[:, :, 0:2 * F1 - F1 // 2]
                shifted = pre[g % 2].rearrange("p (u c) -> p u c", c=2 * F1)[:, :, F1 // 2:2 * F1]
                act.activation(above, shifted, ACT.Gelu).then_inc(h_ready, 1)

            steps = {"k_proj": k_proj, "ln1_turn": lambda b: keep_xnT(b, 1), "f_proj": f_proj, "v_proj": v_proj,
                     "inverse": inverse, "ln2_turn": lambda b: keep_xnT(b, 2), "q_proj": q_proj, "head": head,
                     "ln3_turn": ln3, "logits_up": spread_tokens, "route_top_up": lambda c: route_exp(c, 0), "route_up": lambda c: route(c, 0),
                     "up": up, "route_top_dn": lambda c: route_exp(c, 1), "route_dn": lambda c: route(c, 1),
                     "choose": choose}
            both_halves(lambda b, c: go(steps, b, c), act)

        @block.tensor
        def _(pe):
            pe.wait_ge(fourier_tables, 16 * FOURIER_LOADS)
            for i, s in enumerate((S0, S1, PT)):
                for ct in range(CT):
                    for j in range(2):
                        mm = pe.matmul(s[:, ct * 256:(ct + 1) * 256], wnat[:, i, j, ct * P:(ct + 1) * P],
                                       dft[:, j, :], start=(j == 0), stop=(j == 1))
                mm.then_inc(folded, 1)
            for half in range(2):
                for j in range(2):
                    mm = pe.matmul(TR[:, 4 * half:4 * half + 3], dft[:, j, half * P:(half + 1) * P],
                                   bnat[:, j, :], start=(j == 0), stop=(j == 1))
            mm.then_inc(folded, 1)
            pe.wait_ge(key_tables, 16 * KEY_LOADS)
            pe.wait_ge(bv_spread, 1)
            pe.wait_ge(vals_ones, 2)
            for m in range(PAIRS):
                pe.matmul(O[:, 0:DIM], bv_wide[:, m, :], wo[:, m, :], start=(m == 0), stop=False)
            pe.matmul(O[:, 0:DIM], ones[0:1, :], bo_row, start=False, stop=True).then_inc(folded, 1)
            pe.wait_ge(folded_kept, 5)
            pe.wait_ge(bias_made, 1)

            def k_proj(b, r):
                if r == 0:
                    pe.wait_ge(ctx_loaded, at(b, 16, 16))
                    pe.wait_ge(scores_masked, at(b, 32, 0))
                    pe.wait_ge(probsT_act, at(b, 8, 0))
                    pe.wait_ge(probsT_dve, at(b, 8, 0))
                if r == 3:
                    pe.wait_ge(x2_done, at(b, 1, 0))
                for i in range(2):
                    m = 2 * r + i
                    for ct in range(CT):
                        mm = pe.matmul(k_banks[r][:, i * 256:(i + 1) * 256], wk[:, ct, m * P:(m + 1) * P],
                                       ctxT[:, ct, :], start=(ct == 0), stop=(ct == CT - 1))
                mm.then_inc(proj_done, 1)

            def turn(b, k):
                pe.wait_ge(ln_done[k - 1], at(b, 2, 2))
                if k == 1:
                    pe.wait_ge(pair_kept, at(b, 8, 0))
                else:
                    pe.wait_ge(x1_done, at(b, 2, 2))
                for ct in range(CT):
                    for rt in range(RT):
                        mm = pe.transpose(TR[:, ct * 256 + rt * P:ct * 256 + (rt + 1) * P],
                                          xn[:, rt, ct * P:(ct + 1) * P], ident[:, :])
                mm.then_inc(xn_turned, 1)

            def f_proj(b, i):
                if i == 0:
                    pe.wait_ge(xnT_ready, at(b, 2, 1))
                pe.wait_ge(proj_kept, at(b, 26, 2 * i + 2))
                for half in range(2):
                    for ct in range(CT):
                        mm = pe.matmul((S0, S1, PT)[i][:, half * 256:(half + 1) * 256], wf[:, ct, i, half * P:(half + 1) * P],
                                       xnT[:, ct, :], start=(ct == 0), stop=(ct == CT - 1))
                mm.then_inc(proj_done, 1)

            def v_proj(b, r):
                if r == 0:
                    pe.wait_ge(attn_tables, 16 * ATTN_LOADS)
                pe.wait_ge(proj_kept, at(b, 26, 10 + 2 * r if r < 3 else 15))
                for ct in range(CT):
                    mm = pe.matmul(v_banks[r][:, :], ctxT[:, ct, (r // 2) * P:(r // 2 + 1) * P],
                                   wv[:, ct, (r % 2) * 512:(r % 2 + 1) * 512], start=(ct == 0), stop=(ct == CT - 1))
                mm.then_inc(proj_done, 1)

            def inverse(b):
                pe.wait_ge(Q_ready, at(b, 2, 2))
                pe.wait_ge(proj_kept, at(b, 26, 18))
                for rt in range(RT):
                    for half in range(2):
                        pe.matmul(O[:, rt * 256:(rt + 1) * 256], Q[:, half * 256 + rt * P:half * 256 + (rt + 1) * P],
                                  idft[:, half, :], start=(half == 0), stop=(half == 1))

            def power(b):
                pe.wait_ge(Qsq_ready, at(b, 1, 1))
                for rt in range(RT):
                    for half in range(2):
                        mm = pe.matmul(TR[:, rt:rt + 1], Qsq[:, half * 256 + rt * P:half * 256 + (rt + 1) * P],
                                       bin_weight[:, :], start=(half == 0), stop=(half == 1))
                mm.then_inc(inverse_done, 1)

            def q_proj(b, r):
                if r == 0:
                    pe.wait_ge(xnT_ready, at(b, 2, 2))
                if r == 1:
                    pe.wait_ge(x1_done, at(b, 2, 2))
                elif r == 0:
                    pe.wait_ge(proj_kept, at(b, 26, 17))
                for i in range(2):
                    m = 2 * r + i
                    for ct in range(CT):
                        mm = pe.matmul(q_banks[r][:, i * 256:(i + 1) * 256], wq[:, ct, m * P:(m + 1) * P],
                                       xnT[:, ct, :], start=(ct == 0), stop=(ct == CT - 1))
                mm.then_inc(proj_done, 1)

            def head(b, i):
                e = i - 3
                if 0 <= e < HEADS:
                    if e % 2 == 0:
                        pe.wait_ge(probsT_act, at(b, 8, e // 2 + 1))
                    else:
                        pe.wait_ge(probsT_dve, at(b, 8, e // 2 + 1))
                e = i - 2
                if 0 <= e < HEADS:
                    pe.wait_ge(probs_ready, at(b, 32, 2 * e + 2))
                    for j in range(3):
                        mm = pe.transpose(PT[:, j * P:(j + 1) * P], probs[e % 3][:, j * P:(j + 1) * P], ident[:, :])
                    mm.then_inc(probs_turned, 1)
                if i < HEADS:
                    m, lo = i // 2, (i % 2) * KEY
                    if i % 4 == 0:
                        pe.wait_ge(proj_kept, at(b, 26, 20 + i // 2))
                    pe.matmul(S[i % 2][:, 0:P], qT[lo:lo + KEY, m, 0:P], kT[lo:lo + KEY, m, 0:P], start=True, stop=True)
                    pe.matmul(S[i % 2][:, P:3 * P], qT[lo:lo + KEY, m, P:2 * P], kT[lo:lo + KEY, m, :],
                              start=True, stop=True).then_inc(scores_done, 1)
                e = i - 3
                if 0 <= e < HEADS:
                    m = e // 2
                    if e % 2 == 0 and m >= 2:
                        pe.wait_ge(pair_kept, at(b, 8, m - 1))
                    to, o = X[m % 2], (e % 2) * RT * (KEY + 1)
                    p = probsT[e % 2]
                    pe.matmul(to[:, o:o + KEY + 1], p[:, 0:P], vals[:, 0, e, :], start=True, stop=True)
                    o += KEY + 1
                    pe.matmul(to[:, o:o + KEY + 1], p[:, P:2 * P], vals[:, 0, e, :], start=True, stop=False)
                    pe.matmul(to[:, o:o + KEY + 1], p[:, 2 * P:3 * P], vals[:, 1, e, :], start=False, stop=True)\
                      .then_inc(pv_done, 1)
                if i >= 5 and i % 2 == 1:
                    turn_pair(b, (i - 5) // 2)

            def turn_pair(b, m):
                pe.wait_ge(pair_normed, at(b, 8, m + 1))
                for rt in range(RT):
                    mm = pe.transpose(X[m % 2][:, rt * P:(rt + 1) * P], pair[m % 2][:, rt, :], ident[:, :])
                mm.then_inc(pair_turned, 1)

            def wo_proj(b, rt):
                for m in range(PAIRS):
                    if rt == 0 and m in (0, PAIRS - 1):
                        pe.wait_ge(pair_kept, at(b, 8, PAIRS - 1 if m == 0 else PAIRS))
                    mm = pe.matmul(O[:, rt * 256:(rt + 1) * 256], qT[:, m, rt * P:(rt + 1) * P], wo[:, m, :],
                                   start=(m == 0), stop=(m == PAIRS - 1))
                mm.then_inc(wo_done, 1)

            def ln3(c):
                pe.wait_ge(ln_done[2], at(c, 2, 2))
                for ct in range(CT):
                    for rt in range(RT):
                        mm = pe.transpose(FA[:, ct * 256 + rt * P:ct * 256 + (rt + 1) * P],
                                          xn3[:, rt, ct * P:(ct + 1) * P], ident[:, :])
                mm.then_inc(xn3_turned, 1)

            def logits_up(c):
                pe.wait_ge(xn3T_ready, at(c, 1, 1))
                pe.wait_ge(ffn_tables, 16 * FFN_LOADS)
                for r in range(UP_TOK):
                    for ct in range(CT):
                        n = r * CT + ct
                        rows = xn3T[:, ct, :].rearrange("p (n r) -> p r n", r=UP_TOK)[:, r, :]
                        mm = pe.matmul(G[0:F1, 0:EXPERTS], rows, r_up[:, n, :], start=(n == 0), stop=(n == 2 * UP_TOK - 1))
                mm.then_inc(logits_done, 1)

            def logits_dn(c):
                pe.wait_ge(h_ready, at(c, 32, 32))
                cols = h[:, :].rearrange("p (n two q) -> p two q n", n=TOKENS, two=2)
                for q in range(F1 // 2):
                    mm = pe.matmul(G[0:F1, 0:EXPERTS], cols[:, 0, q, :], r_dn[:, q, :], start=(q == 0), stop=(q == F1 // 2 - 1))
                mm.then_inc(logits_done, 1)

            def route(c, layer):
                pe.wait_ge(route_ready, at(c, 4, 2 * layer + 2))
                pe.matmul(G[:, 128:384], ones[0:F1, :], route_diag[:, :], start=True, stop=True).then_inc(route_spread, 1)

            def up(c, g):
                if g < UP_GROUPS:
                    pe.wait_ge(chosen_act, at(c, GROUPS, g + 1))
                    pe.wait_ge(chosen_dve, at(c, GROUPS, g + 1))
                    pe.wait_ge(chosen_pool, at(c, UP_GROUPS, g + 1))
                    if g == 0:
                        pe.wait_ge(own_act, at(c, 8, 8))
                        pe.wait_ge(own_dve, at(c, 8, 8))
                    pe.matmul(up_F[g % 3][:, 0:B_UP], own[:, g * P:(g + 1) * P], chosen_up[g % UP_SLOTS][:, A_UP:A_UP + B_UP],
                              start=True, stop=True).then_inc(first_done, 1)
                g -= UP_SKEW
                if g >= 0:
                    pe.wait_ge(W_ready, at(c, GROUPS, g + 1))
                    if g >= 2:
                        pe.wait_ge(hidden_in, at(c, 16, g - 1))
                    else:
                        pe.wait_ge(pm_ready, at(c, 6, 4))
                    n = UP_TOK * F1
                    for k in range(TOPK):
                        mm = pe.matmul(G[g % 2 * F1:(g % 2 + 1) * F1, 0:n], up_W(g)[:, k * F1:(k + 1) * F1],
                                       chosen_up[g % UP_SLOTS][:, k * n:(k + 1) * n], start=(k == 0), stop=(k == TOPK - 1))
                    mm.then_inc(second_done, 1)

            def dn_first(c, g):
                pe.wait_ge(chosen_act, at(c, GROUPS, UP_GROUPS + g + 1))
                hold(pe, passed, chosen_dve, at(c, GROUPS, UP_GROUPS + g + 1))
                w = TOPK * D1
                for u in range(DN_TOK // 2):
                    both = h[:, (g * DN_TOK // 2 + u) * 2 * F1:(g * DN_TOK // 2 + u + 1) * 2 * F1]
                    for half, token in enumerate((both[0:F1, 0:F1], both[F1:P, F1 // 2:F1 // 2 + F1])):
                        rows = slice(half * F1, (half + 1) * F1)
                        mm = pe.matmul(F[g % 2][rows, u * w:(u + 1) * w], token,
                                       chosen_dn[g % DN_SLOTS][rows, A_DN + u * w:A_DN + (u + 1) * w], start=True, stop=True)
                mm.then_inc(first_done, 1)

            def dn_second(c, g):
                pe.wait_ge(W_ready, at(c, GROUPS, UP_GROUPS + g + 1))
                if g >= 2:
                    pe.wait_ge(y_kept, at(c, 32, 4 * g - 4))
                else:
                    pe.wait_ge(pm_ready, at(c, 6, 6))
                for u in range(DN_TOK // 2):
                    for k in range(TOPK):
                        n = u * TOPK + k
                        mm = pe.matmul(G[g % 2 * F1:g % 2 * F1 + D1, u * 2 * D1:(u + 1) * 2 * D1], W[g % 2][:, n * D1:(n + 1) * D1],
                                       chosen_dn[g % DN_SLOTS][:, n * 2 * D1:(n + 1) * 2 * D1],
                                       start=(k == 0), stop=(k == TOPK - 1))
                mm.then_inc(second_done, 1)

            def final(c):
                pe.wait_ge(y_kept, at(c, 32, 32))
                for rt in range(RT):
                    for ct in range(CT):
                        mm = pe.transpose(FA[:, rt * 256 + ct * P:rt * 256 + (ct + 1) * P],
                                          yT[:, ct, rt * P:(rt + 1) * P], ident[:, :])
                mm.then_inc(y_turned, 1)

            steps = {"k_proj": k_proj, "ln1_turn": lambda b: turn(b, 1), "f_proj": f_proj, "v_proj": v_proj,
                     "inverse": inverse, "power": power, "ln2_turn": lambda b: turn(b, 2), "q_proj": q_proj, "head": head, "wo": wo_proj,
                     "ln3_turn": ln3, "logits_up": logits_up, "route_up": lambda c: route(c, 0), "up": up,
                     "logits_dn": logits_dn, "route_dn": lambda c: route(c, 1), "dn_first": dn_first,
                     "dn_second": dn_second, "final": final}
            both_halves(lambda b, c: go(steps, b, c), pe)

        @block.vector
        def _(dve):
            dve.wait_ge(key_tables, 16 * KEY_LOADS)
            dve.tensor_copy(bv_wide, spread(bv[:, :], 2, P)).then_inc(bv_spread, 1)

            def ln_moments_of(b, k, src, rts=range(RT)):
                for rt in rts:
                    dve.bn_stats(stats[:, k, rt, :], src[:, rt, :]).then_inc(ln_stats[k], 1)
                for rt in rts:
                    hold(dve, passed, ln_stats[k], at(b, 2, rt + 1))
                    dve.bn_aggr(moments[:, k, rt, :], stats[:, k, rt, :]).then_inc(ln_moments[k], 1)

            def layernorm(b, k, src, dst, rts=range(RT)):
                if 0 in rts:
                    dve.wait_ge(ln_rstd[k], at(b, 2, 2))
                for rt in rts:
                    dve.tensor_scalar(dst[:, rt, :], src[:, rt, :], moments[:, k, rt, 0:1], rstd[:, k, rt:rt + 1],
                                      ALU.subtract, ALU.mult).then_inc(ln_done[k], 1)

            def ln1_stats(b):
                dve.wait_ge(x_loaded, at(b, 16, 16))
                ln_moments_of(b, 0, x)

            def product_kv(b):
                dve.wait_ge(proj_kept, at(b, 26, 12))
                dve.tensor_tensor(prodA, kF, vF, ALU.mult).then_inc(straight, 1)

            def cumulate(b):
                dve.wait_ge(lane_fixed, at(b, 6, 3))
                dve.tensor_tensor_scan(KV[:, 0:256], prodA[:, 0:256], prodA[:, 256:512], 0.0, ALU.add, ALU.subtract)\
                   .then_inc(summed, 1)
                dve.tensor_tensor_scan(KV[:, 256:512], prodB[:, 0:256], prodB[:, 256:512], 0.0, ALU.add, ALU.add)\
                   .then_inc(summed, 1)

            def product_q(b):
                dve.wait_ge(summed, at(b, 2, 2))
                dve.wait_ge(proj_kept, at(b, 26, 14))
                dve.tensor_tensor(prodA, KV, qF, ALU.mult).then_inc(straight, 1)

            def spectrum(b):
                dve.wait_ge(lane_fixed, at(b, 6, 6))
                dve.tensor_tensor(Q[:, 0:256], prodA[:, 0:256], prodA[:, 256:512], ALU.add).then_inc(Q_ready, 1)
                dve.tensor_tensor(Q[:, 256:512], prodB[:, 256:512], prodB[:, 0:256], ALU.subtract).then_inc(Q_ready, 1)

            def fpower_keep(b):
                dve.wait_ge(inverse_done, at(b, 1, 1))
                dve.tensor_copy(fpower[:, :], TR[:, 0:RT]).then_inc(fpower_kept, 1)

            def residual1(b, rt):
                if rt == 0:
                    dve.wait_ge(fnorm_step, at(b, 2, 2))
                    dve.reciprocal(fscale[:, :], fnorm[:, :]).then_inc(fscale_ready, 1)
                    dve.wait_ge(fscale_ready, at(b, 1, 1))
                dve.scalar_tensor_tensor(x1[:, rt, :], O[:, rt * 256:(rt + 1) * 256], fscale[:, rt:rt + 1],
                                         x[:, rt, :], ALU.mult, ALU.add).then_inc(x1_done, 1)

            def ln2_stats(b, rt):
                dve.wait_ge(x1_done, at(b, 2, rt + 1))
                ln_moments_of(b, 1, x1, [rt])

            def head(b, i):
                e = i - 2
                if 0 <= e < HEADS and e % 2 == 1:
                    dve.wait_ge(probs_turned, at(b, 16, e + 1))
                    dve.tensor_copy(probsT[e % 2], PT[:, 0:384]).then_inc(probsT_dve, 1)
                if i < HEADS:
                    hold(dve, passed, scores_done, at(b, 16, i + 1))
                    if i == 0:
                        dve.wait_ge(ffn_tables, 16 * FFN_LOADS)
                    for rt, (lo, hi) in enumerate(((0, 128), (128, 384))):
                        dve.tensor_tensor_reduce(probs[i % 3][:, lo:hi], S[i % 2][:, lo:hi],
                                                 neg_bias[:, i, (1 - rt) * P:2 * P], 1.0, TOP, ALU.add, ALU.min,
                                                 neg_max[:, i % 3, rt:rt + 1]).then_inc(scores_masked, 1)
                e = i - 3
                if 0 <= e < HEADS and e % 2 == 1:
                    m = e // 2
                    dve.wait_ge(pv_done, at(b, 16, e + 1))
                    att = X[m % 2][:, 0:2 * RT * (KEY + 1)].rearrange("p (h t d) -> p h t d", h=2, t=RT)
                    dve.reciprocal(rsum[:, m % 2, :, :], att[:, :, :, KEY]).then_inc(rsum_ready, 1)
                    dve.wait_ge(rsum_ready, at(b, 8, m + 1))
                    dve.tensor_tensor(pair[m % 2].rearrange("p t (h d) -> p h t d", h=2), att[:, :, :, 0:KEY],
                                      spread(rsum[:, m % 2, :, :], 3, KEY), ALU.mult).then_inc(pair_normed, 1)

            def wo_add(b):
                dve.wait_ge(wo_done, at(b, 2, 2))
                dve.wait_ge(x1_biased, at(b, 1, 1))
                dve.wait_ge(out_ready, at(b, 1, 0))
                dve.tensor_tensor(x2[:, :, :], O[:, :].rearrange("p (t c) -> p t c", t=RT), x1[:, :, :], ALU.add)\
                   .then_inc(x2_done, 1)

            def ln3_stats(c):
                dve.wait_ge(x2_done, at(c, 1, 1))
                ln_moments_of(c, 2, x2)

            def ln3(c):
                dve.wait_ge(result_free, at(c, 1, 1))
                layernorm(c, 2, x2, xn3)

            def spread_tokens(c):
                dve.wait_ge(xn3T_ready, at(c, 1, 1))
                dve.wait_ge(zeroed, 1 + UP_SLOTS + DN_SLOTS)
                for n in (2, 3):
                    for il in range(4):
                        dve.tensor_copy(*own_parts(n, il)).then_inc(own_dve, 1)

            def route_top(c, layer):
                step = 2 * F1 if layer == 0 else 2 * D1
                hold(dve, passed, logits_done, at(c, 2, layer + 1))
                dve.max(top_val[:, :], G[0:F1, 0:EXPERTS]).then_inc(top_found, 1)
                dve.wait_ge(top_found, at(c, 4, 2 * layer + 1))
                dve.tensor_tensor(gap[:, :], top_val[:, 1:2], top_val[:, 0:1], ALU.subtract).then_inc(gap_ready, 1)
                dve.max_index(top_idx[:, :], top_val[:, :], G[0:F1, 0:EXPERTS]).then_inc(top_found, 1)
                dve.wait_ge(top_found, at(c, 4, 2 * layer + 2))
                dve.tensor_scalar(place[:, :], top_idx[:, 0:TOPK], float(step), None, ALU.mult).then_inc(route_step, 1)
                dve.wait_ge(gap_exp, at(c, 2, layer + 1))
                dve.tensor_scalar(den[:, :], egap[:, :], 1.0, None, ALU.add).then_inc(route_step, 1)
                dve.wait_ge(route_step, at(c, 8, 4 * layer + 2))
                dve.reciprocal(prob[:, 0:1], den[:, :]).then_inc(route_step, 1)
                dve.wait_ge(route_step, at(c, 8, 4 * layer + 3))
                dve.tensor_tensor(prob[:, 1:2], egap[:, :], prob[:, 0:1], ALU.mult).then_inc(route_step, 1)
                dve.wait_ge(route_step, at(c, 8, 4 * layer + 4))
                eye = spread(ident[0:F1, 0:TOKENS], 2, TOPK)
                for half, val in enumerate((prob, place)):
                    n = TOKENS * TOPK
                    dve.tensor_tensor(route_diag[:, half * n:(half + 1) * n].rearrange("p (n k) -> p n k", k=TOPK), eye,
                                      spread(val[:, :], 1, TOKENS), ALU.mult).then_inc(route_ready, 1)

            def route_keep(c, layer):
                dve.wait_ge(route_spread, at(c, 2, layer + 1))
                n = UP_TOK if layer == 0 else DN_TOK
                groups = TOKENS // n
                of = G[0:1, 256:384].rearrange("p (g u) -> p g u", g=groups)
                for name in CHOOSERS:
                    units, start = share_of(name, "up" if layer == 0 else "dn")
                    if len(units) > 0:
                        to = offsets[:, start:start + groups * len(units)].rearrange("p (g u) -> p g u", g=groups)
                        last = dve.tensor_copy(to, of[:, :, units.start:units.stop])
                last.then_inc(offsets_ready, 1)
                n = UP_TOK if layer == 0 else 2
                width, groups = P // n, TOKENS // n
                for j in range(n):
                    rows = slice(j * width, (j + 1) * width)
                    dve.tensor_copy(pm[rows, 0:groups * TOPK].rearrange("p (g k) -> p g k", k=TOPK),
                                    G[rows, 128:256].rearrange("p (g n k) -> p n g k", n=n, k=TOPK)[:, j])\
                       .then_inc(pm_ready, 1)

            def route(c, layer):
                route_keep(c, layer)
                hold(dve, passed, offsets_ready, at(c, 2, layer + 1))

            held = {}

            def choose(c, n_part):
                n, part = n_part
                layer = "up" if n < UP_GROUPS else "dn"
                units = CHOOSERS["dve"][layer]
                if part == 0:
                    fetch_offsets(held, mybir.EngineType.DVE, n, "dve")
                if n < UP_GROUPS:
                    choose_up(dve.tensor_copy, held, n, units).then_inc(chosen_dve, 1)
                else:
                    g = n - UP_GROUPS
                    cut = len(units) // CHOOSE_PARTS
                    last = choose_dn(dve.tensor_copy, held, g, units[:cut] if part == 0 else units[cut:])
                    if part == CHOOSE_PARTS - 1:
                        last.then_inc(chosen_dve, 1)

            def weigh(c, n, width, per_group):
                up_layer = n < UP_GROUPS
                g = n if up_layer else n - UP_GROUPS
                dve.wait_ge(first_done, at(c, GROUPS, n + 1))
                if g == 0:
                    dve.wait_ge(pm_ready, at(c, 6, 4 if up_layer else 6))
                to, first = (up_W(g), up_F[g % 3][:, 0:B_UP]) if up_layer else (W[g % 2][:, :], F[g % 2][:, 0:A_DN // 2])
                dve.tensor_tensor(to.rearrange("p (s w) -> p s w", w=width), first.rearrange("p (s w) -> p s w", w=width),
                                  spread(pm[:, g * per_group:(g + 1) * per_group], 2, width), ALU.mult).then_inc(W_ready, 1)

            def up(c, g):
                if g < UP_GROUPS:
                    weigh(c, g, F1, TOPK)
                g -= UP_SKEW
                if g >= 0:
                    dve.wait_ge(second_done, at(c, GROUPS, g + 1))
                    if g >= 2:
                        dve.wait_ge(h_ready, at(c, 32, 2 * g - 2))
                    n = UP_TOK * F1
                    side = slice(g % 2 * F1, (g % 2 + 1) * F1)
                    dve.scalar_tensor_tensor(pre[g % 2].rearrange("p (n o) -> p n o", o=F1),
                                             G[side, 0:n].rearrange("p (n o) -> p n o", o=F1),
                                             scale_up[side, 0:1], spread(bias_up[side, :], 1, UP_TOK),
                                             ALU.mult, ALU.add).then_inc(hidden_in, 1)

            def keep_y(c, g):
                dve.wait_ge(second_done, at(c, GROUPS, UP_GROUPS + g + 1))
                rows = DN_TOK * 4
                y = G[g % 2 * F1:g % 2 * F1 + D1, 0:DN_TOK * D1].rearrange("p (s c i) -> p i c s", c=CT, i=4)
                for il in range(4):
                    dve.tensor_copy(yT[il * D1:(il + 1) * D1, :, g * rows:(g + 1) * rows], y[:, il]).then_inc(y_kept, 1)

            def final(c):
                dve.wait_ge(x2_biased, at(c, 1, 1))
                dve.wait_ge(y_turned, at(c, 1, 1))
                dve.scalar_tensor_tensor(xn3[:, :, :], FA[:, :].rearrange("p (t c) -> p t c", t=RT), scale_dn[:, 0:1],
                                         x2[:, :, :], ALU.mult, ALU.add).then_inc(out_ready, 1)

            steps = {"ln1_stats": ln1_stats, "ln1": lambda b: layernorm(b, 0, x, xn), "product_kv": product_kv,
                     "cumulate": cumulate, "product_q": product_q, "Q": spectrum, "fpower": fpower_keep, "x1": residual1,
                     "ln2_stats": ln2_stats, "ln2": lambda b, rt: layernorm(b, 1, x1, xn, [rt]), "head": head, "wo_add": wo_add,
                     "ln3_stats": ln3_stats, "ln3": ln3, "logits_up": spread_tokens,
                     "route_top_up": lambda c: route_top(c, 0), "route_up": lambda c: route(c, 0), "up": up,
                     "route_top_dn": lambda c: route_top(c, 1), "route_dn": lambda c: route(c, 1),
                     "dn_first": lambda c, g: weigh(c, UP_GROUPS + g, D1, DN_TOK // 2 * TOPK), "dn_second": keep_y,
                     "final": final, "choose": choose}
            both_halves(lambda b, c: go(steps, b, c), dve)


def constants():
    n = np.arange(DIM)
    f = np.arange(P)
    angle = 2.0 * np.pi * np.outer(n, f) / DIM
    half = (-1.0) ** n
    dft = np.concatenate([np.cos(angle), -np.sin(angle)], 1)
    dft[:, P] = half
    inv = np.concatenate([2.0 * np.cos(angle), -2.0 * np.sin(angle)], 1)
    inv[:, 0] = 1.0
    inv[:, P] = half
    inv /= DIM * math.sqrt(DIM)
    weight = np.full((P, 1), 2.0)
    weight[0] = 1.0
    start = 2 ** (-2 ** (-(math.log2(HEADS) - 3)))
    slopes = np.array([start * start ** i for i in range(HEADS)], np.float32)
    rel = ((SEQ - P + np.arange(P))[:, None, None] - np.arange(SEQ)[None, None, :]).astype(np.float32)
    alibi = slopes[None, :, None] * rel
    neg_bias = np.where(rel >= 0, -alibi, np.float32(BIG))
    made = {"dft": dft, "idft": inv.T, "bin_weight": weight, "neg_bias": neg_bias, "ident": np.eye(P)}
    return {k: np.ascontiguousarray(v, dtype=np.float32) for k, v in made.items()}


def kernel(**inputs):
    import concourse.bacc as bacc
    from concourse.bass_utils import run_bass_kernel_spmd

    a = {k: np.asarray(v) for k, v in inputs.items()}
    E = EXPERTS

    def columns(v):
        return v.reshape(-1, P).T

    arrays = {
        "x": a["x"],
        "ctxT": a["ctx_1024"].transpose(0, 2, 1),
        "Wk": a["L0_attn_Wk"], "Wv": a["L0_attn_Wv"], "Wq": a["L0_attn_Wq"],
        "b_fourier": np.stack([a[f"L0_attn_b{n}"].reshape(2, P).T for n in "kvq"], 2),
        "xWq": a["L0_xattn_Wq"], "xWk": a["L0_xattn_Wk"], "xWv": a["L0_xattn_Wv"], "xWo": a["L0_xattn_Wo"],
        "xbq": columns(a["L0_xattn_bq"]), "xbk": columns(a["L0_xattn_bk"]), "xbv": columns(a["L0_xattn_bv"]),
        "xbo": a["L0_xattn_bo"][None, :],
        "r_up": a["L0_ffn_W_up"].T.reshape(UP_TOK * CT, P, E).transpose(1, 0, 2),
        "r_dn": a["L0_ffn_W_down"].reshape(E, 2, F1 // 2, F1).transpose(1, 3, 2, 0).reshape(P, F1 // 2, E),
        "experts_up": np.stack([a["L0_ffn_A_up"], a["L0_ffn_B_up"]], 1).transpose(3, 0, 1, 2).reshape(D1, -1),
        "experts_dn": np.stack([a["L0_ffn_A_down"], a["L0_ffn_B_down"]], 1).transpose(3, 0, 1, 2).reshape(F1, -1),
        "bias_up": np.tile(a["L0_ffn_bias_up"].reshape(F1, F1).T, (2, 1)),
        "bias_dn": np.tile(a["L0_ffn_bias_down"].reshape(4, DIM), (P // 4, 1)),
        "scale_up": a["L0_ffn_scale_up"].reshape(1, 1), "scale_dn": a["L0_ffn_scale_down"].reshape(1, 1),
        **constants(),
    }
    arrays = {k: np.ascontiguousarray(v) for k, v in arrays.items()}
    nc = bacc.Bacc("TRN2", target_bir_lowering=False, num_devices=1)
    t = {k: nc.dram_tensor(f"in_{k}", v.shape, mybir.dt.from_np(v.dtype), kind="ExternalInput").ap() for k, v in arrays.items()}
    out = nc.dram_tensor("out", (BATCH, SEQ, DIM), F32, kind="ExternalOutput").ap()
    decoder_layer(nc, t, out)
    r = run_bass_kernel_spmd(nc, [{f"in_{k}": v for k, v in arrays.items()}], core_ids=[0])
    return r.results[0]["out"]
```
